# Optimizing a Trainium2 kernel written in Bass

```python
import numpy as np
import jax
import jax.numpy as jnp

def _softmax(x, axis=-1):
    return jax.nn.softmax(x, axis=axis)

def _gelu(x):
    return jax.nn.gelu(x, approximate=True)

def _silu(x):
    return jax.nn.silu(x)

def _sigmoid(x):
    return jax.nn.sigmoid(x)

def _layernorm(x, axis=-1, eps=1e-05):
    m = jnp.mean(x, axis=axis, keepdims=True)
    v = jnp.var(x, axis=axis, keepdims=True)
    return (x - m) / jnp.sqrt(v + eps)

def _scatter_add(tgt, idx, src, axis=0):
    return tgt.at[idx].add(src)

def _segment_sum(src, seg, n):
    return jax.ops.segment_sum(src, seg, n)
kernel_name = 'mk_seq_postln_d1_jaxref_r8_38d937'

def setup_inputs(seed: int=0):
    np.random.seed(seed)
    _w = jnp.asarray

    def _L0_attn_setup():
        import jax, jax.numpy as jnp
        import numpy as np
        B, T, D_IN, D_STATE = (4, 512, 128, 256)
        key = jax.random.key(seed)
        k_u, k_wi, k_wo = jax.random.split(key, 3)
        u = jax.random.normal(k_u, (B, T, D_IN), dtype=jnp.float32)
        W_in = jax.random.normal(k_wi, (D_STATE, D_IN), dtype=jnp.float32) / np.sqrt(D_IN)
        W_out = jax.random.normal(k_wo, (D_IN, D_STATE), dtype=jnp.float32) / np.sqrt(D_STATE)
        log_lambda = jnp.ones((D_STATE,), dtype=jnp.float32) * 2.0
        D = jnp.ones((D_IN,), dtype=jnp.float32) * 0.1
        return {'u': u, 'W_in': W_in, 'log_lambda': log_lambda, 'W_out': W_out, 'D': D}
    _L0_attn_in = _L0_attn_setup()

    def _L0_ffn_setup():
        import jax, jax.numpy as jnp
        import numpy as np
        DIM = 128
        NQ = 16
        NKV = 4
        HD = DIM // NQ
        HID = 256
        E = 8
        B, S = (1, 128)
        EPS = 1e-06

        def rmsnorm(x, w):
            ms = jnp.mean(x * x, axis=-1, keepdims=True)
            return w * (x * jax.lax.rsqrt(ms + EPS))

        def rope_tables(seq_len, head_dim):
            inv_freq = 1.0 / 10000.0 ** (jnp.arange(0, head_dim, 2, dtype=jnp.float32) / head_dim)
            t = jnp.arange(seq_len, dtype=jnp.float32)
            freqs = jnp.einsum('i,j->ij', t, inv_freq)
            return (jnp.cos(freqs), jnp.sin(freqs))

        def apply_rope(x, cos, sin):
            c = cos[None, :, None, :]
            s = sin[None, :, None, :]
            half = x.shape[-1] // 2
            x1, x2 = (x[..., :half], x[..., half:])
            return jnp.concatenate([x1 * c - x2 * s, x1 * s + x2 * c], axis=-1)

        def _forward(x, ln1_w, ln2_w, Wq, bq, Wk, bk, Wv, bv, qn_w, kn_w, Wg, bg, Wo, bo, Wr, br, W1, b1, W2, b2):
            batch, seq, _ = x.shape
            cos, sin = rope_tables(seq, HD)
            h = rmsnorm(x, ln1_w)
            q = (h @ Wq + bq).reshape(batch, seq, NQ, HD)
            k = (h @ Wk + bk).reshape(batch, seq, NKV, HD)
            v = (h @ Wv + bv).reshape(batch, seq, NKV, HD)
            q = rmsnorm(apply_rope(q, cos, sin), qn_w)
            k = rmsnorm(apply_rope(k, cos, sin), kn_w)
            rep = NQ // NKV
            k = jnp.repeat(k, rep, axis=2)
            v = jnp.repeat(v, rep, axis=2)
            scores = jnp.einsum('bthd,bshd->bhts', q, k) / np.sqrt(HD)
            causal = jnp.tril(jnp.ones((seq, seq), dtype=bool))
            scores = jnp.where(causal[None, None], scores, -jnp.inf)
            attn = jax.nn.softmax(scores, axis=-1)
            out = jnp.einsum('bhts,bshd->bthd', attn, v)
            gate = jax.nn.sigmoid(out @ Wg + bg)
            out = (out * gate).reshape(batch, seq, DIM)
            x = x + out @ Wo + bo
            h2 = rmsnorm(x, ln2_w)
            logits = h2 @ Wr + br
            top1 = jnp.argmax(logits, axis=-1).reshape(-1)
            xt = h2.reshape(-1, DIM)
            u = jnp.einsum('td,edf->tef', xt, W1) + b1
            u1, u2 = (u[..., :HID], u[..., HID:])
            act = u1 * jax.nn.sigmoid(u2)
            y_all = jnp.einsum('teh,ehd->ted', act, W2) + b2
            y = jnp.take_along_axis(y_all, top1[:, None, None], axis=1)[:, 0, :]
            return x + y.reshape(batch, seq, DIM)
        key = jax.random.key(seed)
        ks = jax.random.split(key, 20)
        sc = lambda fan_in: 1.0 / np.sqrt(fan_in)
        d = {}
        d['x'] = jax.random.normal(ks[0], (B, S, DIM), dtype=jnp.float32)
        d['ln1_w'] = jnp.ones((DIM,), jnp.float32)
        d['ln2_w'] = jnp.ones((DIM,), jnp.float32)
        d['Wq'] = jax.random.normal(ks[1], (DIM, DIM), jnp.float32) * sc(DIM)
        d['bq'] = jnp.zeros((DIM,), jnp.float32)
        d['Wk'] = jax.random.normal(ks[2], (DIM, HD * NKV), jnp.float32) * sc(DIM)
        d['bk'] = jnp.zeros((HD * NKV,), jnp.float32)
        d['Wv'] = jax.random.normal(ks[3], (DIM, HD * NKV), jnp.float32) * sc(DIM)
        d['bv'] = jnp.zeros((HD * NKV,), jnp.float32)
        d['qn_w'] = jnp.ones((HD,), jnp.float32)
        d['kn_w'] = jnp.ones((HD,), jnp.float32)
        d['Wg'] = jax.random.normal(ks[4], (HD, HD), jnp.float32) * sc(HD)
        d['bg'] = jnp.zeros((HD,), jnp.float32)
        d['Wo'] = jax.random.normal(ks[5], (DIM, DIM), jnp.float32) * sc(DIM)
        d['bo'] = jnp.zeros((DIM,), jnp.float32)
        d['Wr'] = jax.random.normal(ks[6], (DIM, E), jnp.float32) * sc(DIM)
        d['br'] = jnp.zeros((E,), jnp.float32)
        d['W1'] = jax.random.normal(ks[7], (E, DIM, 2 * HID), jnp.float32) * sc(DIM)
        d['b1'] = jnp.zeros((E, 2 * HID), jnp.float32)
        d['W2'] = jax.random.normal(ks[8], (E, HID, DIM), jnp.float32) * sc(HID)
        d['b2'] = jnp.zeros((E, DIM), jnp.float32)
        return d
    _L0_ffn_in = _L0_ffn_setup()
    _d = {'L0_attn_u': _L0_attn_in['u'], 'L0_attn_W_in': _L0_attn_in['W_in'], 'L0_attn_log_lambda': _L0_attn_in['log_lambda'], 'L0_attn_W_out': _L0_attn_in['W_out'], 'L0_attn_D': _L0_attn_in['D'], 'L0_ffn_ln1_w': _L0_ffn_in['ln1_w'], 'L0_ffn_ln2_w': _L0_ffn_in['ln2_w'], 'L0_ffn_Wq': _L0_ffn_in['Wq'], 'L0_ffn_bq': _L0_ffn_in['bq'], 'L0_ffn_Wk': _L0_ffn_in['Wk'], 'L0_ffn_bk': _L0_ffn_in['bk'], 'L0_ffn_Wv': _L0_ffn_in['Wv'], 'L0_ffn_bv': _L0_ffn_in['bv'], 'L0_ffn_qn_w': _L0_ffn_in['qn_w'], 'L0_ffn_kn_w': _L0_ffn_in['kn_w'], 'L0_ffn_Wg': _L0_ffn_in['Wg'], 'L0_ffn_bg': _L0_ffn_in['bg'], 'L0_ffn_Wo': _L0_ffn_in['Wo'], 'L0_ffn_bo': _L0_ffn_in['bo'], 'L0_ffn_Wr': _L0_ffn_in['Wr'], 'L0_ffn_br': _L0_ffn_in['br'], 'L0_ffn_W1': _L0_ffn_in['W1'], 'L0_ffn_b1': _L0_ffn_in['b1'], 'L0_ffn_W2': _L0_ffn_in['W2'], 'L0_ffn_b2': _L0_ffn_in['b2']}
    _x0 = _d['L0_attn_u']
    _d['L0_attn_u'] = jax.random.normal(jax.random.fold_in(jax.random.key(seed), 1), (4, 1024, 128), dtype=_x0.dtype)
    del _x0
    return _d

def reference(L0_attn_u, L0_attn_W_in, L0_attn_log_lambda, L0_attn_W_out, L0_attn_D, L0_ffn_ln1_w, L0_ffn_ln2_w, L0_ffn_Wq, L0_ffn_bq, L0_ffn_Wk, L0_ffn_bk, L0_ffn_Wv, L0_ffn_bv, L0_ffn_qn_w, L0_ffn_kn_w, L0_ffn_Wg, L0_ffn_bg, L0_ffn_Wo, L0_ffn_bo, L0_ffn_Wr, L0_ffn_br, L0_ffn_W1, L0_ffn_b1, L0_ffn_W2, L0_ffn_b2):

    def _L0_attn_ref(u, W_in, log_lambda, W_out, D):
        import jax, jax.numpy as jnp
        import numpy as np
        B, T, D_IN, D_STATE = (4, 512, 128, 256)
        lam = jax.nn.sigmoid(log_lambda)
        u_proj = jnp.einsum('btd,sd->bts', u, W_in)

        def step(x, up_t):
            x = lam * x + (1.0 - lam) * up_t
            return (x, x)
        x0 = jnp.zeros((u.shape[0], W_in.shape[0]), dtype=u.dtype)
        _, xs = jax.lax.scan(step, x0, jnp.swapaxes(u_proj, 0, 1))
        xs = jnp.swapaxes(xs, 0, 1)
        y = jnp.einsum('bts,ds->btd', xs, W_out) + u * D
        return y

    def _L0_ffn_ref(x, ln1_w, ln2_w, Wq, bq, Wk, bk, Wv, bv, qn_w, kn_w, Wg, bg, Wo, bo, Wr, br, W1, b1, W2, b2):
        import jax, jax.numpy as jnp
        import numpy as np
        DIM = 128
        NQ = 16
        NKV = 4
        HD = DIM // NQ
        HID = 256
        E = 8
        B, S = (1, 128)
        EPS = 1e-06

        def rmsnorm(x, w):
            ms = jnp.mean(x * x, axis=-1, keepdims=True)
            return w * (x * jax.lax.rsqrt(ms + EPS))

        def rope_tables(seq_len, head_dim):
            inv_freq = 1.0 / 10000.0 ** (jnp.arange(0, head_dim, 2, dtype=jnp.float32) / head_dim)
            t = jnp.arange(seq_len, dtype=jnp.float32)
            freqs = jnp.einsum('i,j->ij', t, inv_freq)
            return (jnp.cos(freqs), jnp.sin(freqs))

        def apply_rope(x, cos, sin):
            c = cos[None, :, None, :]
            s = sin[None, :, None, :]
            half = x.shape[-1] // 2
            x1, x2 = (x[..., :half], x[..., half:])
            return jnp.concatenate([x1 * c - x2 * s, x1 * s + x2 * c], axis=-1)

        def _forward(x, ln1_w, ln2_w, Wq, bq, Wk, bk, Wv, bv, qn_w, kn_w, Wg, bg, Wo, bo, Wr, br, W1, b1, W2, b2):
            batch, seq, _ = x.shape
            cos, sin = rope_tables(seq, HD)
            h = rmsnorm(x, ln1_w)
            q = (h @ Wq + bq).reshape(batch, seq, NQ, HD)
            k = (h @ Wk + bk).reshape(batch, seq, NKV, HD)
            v = (h @ Wv + bv).reshape(batch, seq, NKV, HD)
            q = rmsnorm(apply_rope(q, cos, sin), qn_w)
            k = rmsnorm(apply_rope(k, cos, sin), kn_w)
            rep = NQ // NKV
            k = jnp.repeat(k, rep, axis=2)
            v = jnp.repeat(v, rep, axis=2)
            scores = jnp.einsum('bthd,bshd->bhts', q, k) / np.sqrt(HD)
            causal = jnp.tril(jnp.ones((seq, seq), dtype=bool))
            scores = jnp.where(causal[None, None], scores, -jnp.inf)
            attn = jax.nn.softmax(scores, axis=-1)
            out = jnp.einsum('bhts,bshd->bthd', attn, v)
            gate = jax.nn.sigmoid(out @ Wg + bg)
            out = (out * gate).reshape(batch, seq, DIM)
            x = x + out @ Wo + bo
            h2 = rmsnorm(x, ln2_w)
            logits = h2 @ Wr + br
            top1 = jnp.argmax(logits, axis=-1).reshape(-1)
            xt = h2.reshape(-1, DIM)
            u = jnp.einsum('td,edf->tef', xt, W1) + b1
            u1, u2 = (u[..., :HID], u[..., HID:])
            act = u1 * jax.nn.sigmoid(u2)
            y_all = jnp.einsum('teh,ehd->ted', act, W2) + b2
            y = jnp.take_along_axis(y_all, top1[:, None, None], axis=1)[:, 0, :]
            return x + y.reshape(batch, seq, DIM)
        return _forward(x, ln1_w, ln2_w, Wq, bq, Wk, bk, Wv, bv, qn_w, kn_w, Wg, bg, Wo, bo, Wr, br, W1, b1, W2, b2)
    x = L0_attn_u
    x = _layernorm(x + _L0_attn_ref(x, L0_attn_W_in, L0_attn_log_lambda, L0_attn_W_out, L0_attn_D), axis=-1)
    x = _layernorm(x + _L0_ffn_ref(x, L0_ffn_ln1_w, L0_ffn_ln2_w, L0_ffn_Wq, L0_ffn_bq, L0_ffn_Wk, L0_ffn_bk, L0_ffn_Wv, L0_ffn_bv, L0_ffn_qn_w, L0_ffn_kn_w, L0_ffn_Wg, L0_ffn_bg, L0_ffn_Wo, L0_ffn_bo, L0_ffn_Wr, L0_ffn_br, L0_ffn_W1, L0_ffn_b1, L0_ffn_W2, L0_ffn_b2), axis=-1)
    return x

_drawn_inputs = setup_inputs


def setup_inputs(seed=0):
    import zlib

    import numpy as np

    out = dict(_drawn_inputs(seed))
    spreads = {'L0_attn_log_lambda': (2.0, 0.2),
     'L0_attn_D': (0.10000000149011612, 0.2),
     'L0_ffn_ln1_w': (1.0, 0.2),
     'L0_ffn_ln2_w': (1.0, 0.2),
     'L0_ffn_bq': (0.0, 0.1),
     'L0_ffn_bk': (0.0, 0.303),
     'L0_ffn_bv': (0.0, 0.1),
     'L0_ffn_qn_w': (1.0, 0.2),
     'L0_ffn_kn_w': (1.0, 0.2),
     'L0_ffn_bg': (0.0, 0.309),
     'L0_ffn_bo': (0.0, 0.1),
     'L0_ffn_br': (0.0, 0.1),
     'L0_ffn_b1': (0.0, 0.285),
     'L0_ffn_b2': (0.0, 0.1)}
    factors = {}
    for name, (base, spread) in spreads.items():
        noise = np.random.default_rng([zlib.crc32(name.encode()), seed]).standard_normal(out[name].shape)
        drawn = base * np.exp(spread * noise) if base else spread * noise
        out[name] = jnp.asarray(drawn.astype(out[name].dtype))
    for name, factor in factors.items():
        out[name] = (out[name] * factor).astype(out[name].dtype)
    return out
```

```python
from contextlib import ExitStack

import numpy as np

import concourse.bass as bass
from concourse import mybir

F32 = mybir.dt.float32
BF16 = mybir.dt.bfloat16
I32 = mybir.dt.int32
ALU = mybir.AluOpType
ACT = mybir.ActivationFunctionType
AX_X = mybir.AxisListType.X

P = 128
B, T, D = 4, 1024, 128
STATE = 256
SH = STATE // P
NQ, NKV, HD = 16, 4, 8
GH = NQ // NKV
QW, KW = NQ * HD, NKV * HD
HID, E = 256, 8
LN_EPS, RMS_EPS = 1e-5, 1e-6
CH = 512
NC = T // CH
TQ = CH // P
NT = T // P
CHUNKS = B * NC
RSQRT_MAGIC = float(0x5F3759DF)
SHIFT_FROM = 60.0

PARTS = 3
TERMS = PARTS * PARTS

RH = 2 * HD
RCOLS = GH * RH + GH


def attention_units():
    units, subs = [], []
    for g in range(NKV):
        for c in range(NC):
            last = TQ * (c + 1) - 1
            for i in range(last + 1):
                width = CH - P * max(0, i - TQ * c)
                unit = dict(g=g, c=c, i=i, w=width, diag=i >= TQ * c, first=i == 0, last=i == last, subs=[])
                heads = [(0, 1), (2, 3)] if width > CH // 2 else [(0, 1, 2, 3)]
                for hs in heads:
                    unit["subs"].append(len(subs))
                    subs.append((len(units), hs))
                units.append(unit)
    n = 0
    for u in units:
        u["masks_before"] = n
        n += u["diag"]
    return units, subs


UNITS, SUBS = attention_units()
NU, NS, NM = len(UNITS), len(SUBS), sum(u["diag"] for u in UNITS)
PROBS = 3
assert NU % PROBS == 0 and NS % 2 == 0


def block_kernel(nc, uT, WinT, log_lambda, WoutT, Dvec, ln1_w, ln2_w, Wq, bq, Wk, bk, Wv, bv, qn_w, kn_w,
                 gate_mix, bg, Wo, bo, Wr, br, W1, b1, W2, b2, ident, cos8, sin8, first_of, out):
    with ExitStack() as ctx:
        def sb(name, shape, dt=F32):
            return ctx.enter_context(nc.sbuf_tensor(name, shape, dt))

        def sem(name):
            return ctx.enter_context(nc.semaphore(name))

        w_in = sb("w_in", [P, STATE])
        w_out = sb("w_out", [P, SH, D])
        log_lam = sb("log_lam", [P, SH])
        lam = sb("lam", [P, SH])
        one_minus_lam = sb("one_minus_lam", [P, SH])
        d_col = sb("d_col", [P, 1])
        skip_diag = sb("skip_diag", [P, P])
        idm = sb("idm", [P, P])
        ln1_col = sb("ln1_col", [P, 1])
        ln2_col = sb("ln2_col", [P, 1])
        w_qkv = sb("w_qkv", [P, QW + 2 * KW])
        b_qkv = sb("b_qkv", [P, QW + 2 * KW])
        qn_col = sb("qn_col", [P, 1])
        kn_col = sb("kn_col", [KW, 1])
        norm_rows = sb("norm_rows", [P, 2, HD])
        bound = sb("bound", [P, HD])
        shift = sb("shift", [P, 1])
        mix = sb("mix", [P, RCOLS])
        bg_b = sb("bg_b", [P, NQ, HD])
        w_o = sb("w_o", [P, D])
        bo_b = sb("bo_b", [P, D])
        w_r = sb("w_r", [P, E])
        br_b = sb("br_b", [P, E])
        rank8 = sb("rank8", [P, E])
        w_1 = sb("w_1", [P, E, 2 * HID])
        b_1 = sb("b_1", [P, E, 4])
        w_2 = sb("w_2", [P, E, 2, D])
        b_2 = sb("b_2", [1, E, D])
        ones = sb("ones", [1, P])
        cos_t = sb("cos_t", [P, NT, HD])
        sin_t = sb("sin_t", [P, NT, HD])

        u_sb = sb("u_sb", [P, NC, CH])
        drive = sb("drive", [P, SH, CH])
        xs = sb("xs", [P, NC, SH, CH])
        stats = sb("stats", [P, TQ, 6])
        mv = sb("mv", [P, TQ, 2])
        ln_arg = sb("ln_arg", [P, 2 * TQ])
        ln_rs = sb("ln_rs", [P, 2 * TQ])
        ln_tmp = sb("ln_tmp", [P, 2 * TQ])
        r1 = sb("r1", [P, TQ])
        x1 = sb("x1", [P, TQ, D])
        x1T = sb("x1T", [P, CH])
        qkv = sb("qkv", [P, TQ, QW + 2 * KW])
        rot_a = sb("rot_a", [P, TQ, QW + KW])
        rot_b = sb("rot_b", [P, TQ, QW + KW])
        hs_arg = sb("hs_arg", [P, TQ * (NQ + NKV)])
        hs_rs = sb("hs_rs", [P, TQ * (NQ + NKV)])
        hs_tmp = sb("hs_tmp", [P, TQ * (NQ + NKV)])
        qn = sb("qn", [P, TQ, QW])
        kn = sb("kn", [P, TQ, KW])
        q_scaled = sb("q_scaled", [P, CH])
        k_scaled = sb("k_scaled", [KW, CH])
        q_rest = sb("q_rest", [P, CH])
        k_rest = sb("k_rest", [KW, CH])
        q_parts = sb("q_parts", [P, PARTS, T], BF16)
        k_parts = sb("k_parts", [KW, PARTS, T], BF16)
        resid = sb("resid", [P, B * NT, D])

        q_spill = nc.dram_tensor("q_spill", (PARTS, HD, NQ, T), BF16, kind="Internal").ap()
        k_spill = nc.dram_tensor("k_spill", (NKV, PARTS, HD, T), BF16, kind="Internal").ap()

        qT = sb("qT", [P, NQ, T], BF16)
        kT = sb("kT", [P, NKV, T], BF16)
        v_pad = sb("v_pad", [P, NT, NKV, 32])
        probs = sb("probs", [P, PROBS, GH, CH])
        oT = sb("oT", [P, NKV, T])

        r_den = sb("r_den", [P, NQ])
        o_n = sb("o_n", [P, TQ, NQ, HD])
        gate = sb("gate", [P, TQ, NQ, HD])
        og = sb("og", [P, TQ, QW])
        ogT = sb("ogT", [P, CH])
        x2 = sb("x2", [P, TQ, D])
        sq = sb("sq", [P, TQ, D])
        r2_arg = sb("r2_arg", [P, TQ])
        r2 = sb("r2", [P, TQ])
        r2_tmp = sb("r2_tmp", [P, TQ])
        h2 = sb("h2", [P, TQ, D])
        h2T = sb("h2T", [P, CH])
        h2T_all = nc.dram_tensor("h2T_all", (CHUNKS, P, CH), F32, kind="Internal").ap()
        lg = sb("lg", [P, TQ, E])
        lg_max = sb("lg_max", [P, TQ])
        onehot = sb("onehot", [P, B * NT, E])

        sig = probs[:, 2, 0:2, :]
        actT = probs[:, 0:2, 0:2, :]
        tokT = h2T
        acc = sb("acc", [P, TQ, D])
        y_out = h2

        S2 = [ctx.enter_context(nc.psum_tensor(f"scores{i}", [P, 2, CH], F32)) for i in range(2)]
        O = [ctx.enter_context(nc.psum_tensor(f"outputs{i}", [P, CH], F32)) for i in range(2)]
        M = [ctx.enter_context(nc.psum_tensor(f"misc{i}", [P, CH], F32)) for i in range(2)]
        UP = [[S2[f][:, k, :] for k in range(2)] for f in range(2)]
        Y = O[0]

        w_loaded = sem("w_loaded")
        u_loaded = [sem(f"u_loaded{c}") for c in range(NC)]
        w_scaled = sem("w_scaled")
        zeroed = sem("zeroed")
        misc_full = [sem(f"misc_full{i}") for i in range(2)]
        misc_read = [sem(f"misc_read{i}") for i in range(2)]
        scan_done = sem("scan_done")
        dve_step = sem("dve_step")
        pool_step = sem("pool_step")
        pool_held = sem("pool_held")
        dve_held = sem("dve_held")
        qkn_ready = sem("qkn_ready")
        rot_b_ready = sem("rot_b_ready")
        x1_kept = sem("x1_kept")
        parts_ready = sem("parts_ready")
        v_ready = sem("v_ready")
        spilled = sem("spilled")
        stacked = sem("stacked")
        scores_ready = sem("scores_ready")
        scores_read = sem("scores_read")
        probs_masked = sem("probs_masked")
        probs_used = sem("probs_used")
        o_read = sem("o_read")
        gate_ready = sem("gate_ready")
        gate_exp = sem("gate_exp")
        og_ready = sem("og_ready")
        h2_ready = sem("h2_ready")
        h2T_kept = sem("h2T_kept")
        exp_neg = sem("exp_neg")
        tok_loaded = sem("tok_loaded")
        up_ready = sem("up_ready")
        sig_ready = sem("sig_ready")
        act_ready = sem("act_ready")
        y_ready = sem("y_ready")
        y_read = sem("y_read")
        y_final = sem("y_final")
        stored = sem("stored")

        def uses_a(b, c):
            return b * (8 * NC) + 4 * c

        def uses_c(b, c):
            return b * (8 * NC) + 4 * NC + 4 * c

        row = lambda ap, n: ap.rearrange("(a n) -> a n", a=1).to_broadcast([n, ap.shape[0]])
        col = lambda ap: ap.rearrange("(p a) -> p a", a=1)

        W_DMAS = [
            (w_in[:], WinT), (w_out[:], WoutT.rearrange("(k p) d -> p k d", p=P)),
            (log_lam[:], log_lambda.rearrange("(k p) -> p k", p=P)), (d_col[:], col(Dvec)),
            (idm[:], ident), (ln1_col[:], col(ln1_w)), (ln2_col[:], col(ln2_w)),
            (w_qkv[:, 0:QW], Wq), (w_qkv[:, QW:QW + KW], Wk), (w_qkv[:, QW + KW:], Wv),
            (b_qkv[:, 0:QW], row(bq, P)), (b_qkv[:, QW:QW + KW], row(bk, P)), (b_qkv[:, QW + KW:], row(bv, P)),
            (norm_rows[:, 0, :], row(qn_w, P)), (norm_rows[:, 1, :], row(kn_w, P)),
            (mix[:], gate_mix), (w_o[:], Wo), (bo_b[:], row(bo, P)), (w_r[:], Wr), (br_b[:], row(br, P)),
            (rank8[:], row(first_of, P)), (w_1[:], W1.rearrange("e p f -> p e f")),
            (b_1[:], b1.rearrange("e (f p) -> p e f", p=P)), (w_2[:], W2.rearrange("e (k p) d -> p e k d", p=P)),
            (b_2[:], b2.rearrange("(a e) d -> a e d", a=1)), (cos_t[:], cos8), (sin_t[:], sin8),
        ] + [(qn_col[HD * h:HD * h + HD, :], col(qn_w)) for h in range(NQ)] \
          + [(kn_col[HD * h:HD * h + HD, :], col(kn_w)) for h in range(NKV)] \
          + [(bg_b[:, h, :], row(bg, P)) for h in range(NQ)]

        block = ctx.enter_context(nc.Block())

        SPILLS = 2 * PARTS * 16

        @block.sync
        def _(sp):
            for dst, src in W_DMAS:
                sp.dma_start(dst, src, allow_slow_non_contiguous=True).then_inc(w_loaded, 16)
            with sp.Fori(0, B) as b:
                for c in range(NC):
                    sp.wait_ge(misc_read[0], uses_a(b, 0))
                    sp.dma_start(u_sb[:, c, :], uT[b, :, CH * c:CH * c + CH]).then_inc(u_loaded[c], 16)
                sp.wait_ge(zeroed, 1)
                sp.wait_ge(parts_ready, b * NC + NC)
                for p in range(PARTS):
                    sp.dma_start(q_spill[p].rearrange("d h t -> h d t"), q_parts[:, p, :]).then_inc(spilled, 16)
                    sp.dma_start(k_spill[:, p], k_parts[:, p, :]).then_inc(spilled, 16)
                sp.wait_ge(spilled, b * SPILLS + SPILLS)
                for g in range(NKV):
                    for p in range(PARTS):
                        src = q_spill[p:p + 1, :, GH * g:GH * g + GH, :].rearrange("a d h t -> a d (h t)")
                        sp.dma_start(qT[HD * PARTS * p:HD * PARTS * (p + 1), GH * g:GH * g + GH, :],
                                     src.to_broadcast([PARTS, HD, GH * T])).then_inc(stacked, 16)
                    src = k_spill[g:g + 1].rearrange("a p d t -> a (p d) t")
                    sp.dma_start(kT[0:HD * TERMS, g, :], src.to_broadcast([PARTS, PARTS * HD, T])).then_inc(stacked, 16)
                for c in range(NC):
                    sp.wait_ge(misc_read[0], uses_c(b, c) + 4)
                    sp.dma_start(h2T_all[bass.ds(b * NC + c, 1), :, :].rearrange("a p t -> (a p) t"), h2T[:]).then_inc(h2T_kept, 16)
            sp.wait_ge(h2T_kept, 16 * CHUNKS)
            sp.wait_ge(misc_full[1], uses_c(B - 1, NC - 1) + 4)
            with sp.Fori(0, CHUNKS) as n:
                sp.wait_ge(up_ready, n * (2 * E))
                sp.dma_start(tokT[:], h2T_all[bass.ds(n, 1), :, :].rearrange("a p t -> (a p) t")).then_inc(tok_loaded, 16)
                sp.wait_ge(y_final, n + 1)
                sp.dma_start(out[n], y_out[:]).then_inc(stored, 16)
            sp.wait_ge(stored, 16 * CHUNKS)

        STACK_DMAS = NKV * (PARTS + 1)

        @block.gpsimd
        def _(pool):
            steps = [0, 0]

            def link(ins, b=None, per=0):
                ins.then_inc(pool_step, 1)
                steps[0] += 1
                pool.wait_ge(pool_step, steps[0] if b is None else b * per + steps[0])

            def hold():
                pool.sem_inc(pool_held, 1)

            link(nc.gpsimd.memset(qT[:], 0.0))
            link(nc.gpsimd.memset(kT[:], 0.0))
            link(nc.gpsimd.memset(v_pad[:], 0.0))
            nc.gpsimd.memset(v_pad[:, :, :, HD:HD + 1], 1.0).then_inc(zeroed, 1)
            base = steps[0]
            with pool.Fori(0, B) as b:
                steps[0] = base
                for c in range(NC):
                    U = uses_a(b, c)
                    span = slice(CH * c, CH * c + CH)
                    pool.wait_ge(w_loaded, 16 * len(W_DMAS))
                    pool.wait_ge(misc_read[0], U + 2)
                    hold()
                    nc.gpsimd.tensor_copy(resid[:, bass.ds(b * NT + TQ * c, TQ), :], x1[:]).then_inc(x1_kept, 1)
                    pool.wait_ge(misc_read[0], U + 3)
                    pool.wait_ge(misc_read[1], U + 3)
                    hold()
                    for g in range(NKV):
                        nc.gpsimd.tensor_copy(v_pad[:, TQ * c:TQ * c + TQ, g, 0:HD],
                                              qkv[:, :, QW + KW + HD * g:QW + KW + HD * g + HD]).then_inc(v_ready, 1)
                    for q in range(TQ):
                        qk = qkv[:, q, 0:QW + KW].rearrange("p (h d) -> p h d", d=HD)
                        rb = rot_b[:, q, :].rearrange("p (h d) -> p h d", d=HD)
                        s = sin_t[:, TQ * c + q, :].unsqueeze(1).to_broadcast([P, NQ + NKV, HD])
                        nc.gpsimd.tensor_tensor(rb[:, :, 0:4], qk[:, :, 4:8], s[:, :, 0:4], ALU.mult)
                        last = nc.gpsimd.tensor_tensor(rb[:, :, 4:8], qk[:, :, 0:4], s[:, :, 4:8], ALU.mult)
                    last.then_inc(rot_b_ready, 1)
                    pool.wait_ge(misc_read[0], U + 4)
                    pool.wait_ge(misc_read[1], U + 4)
                    pool.wait_ge(stacked, b * (16 * STACK_DMAS))
                    for x, rest, parts in ((q_scaled, q_rest, q_parts), (k_scaled, k_rest, k_parts)):
                        hold()
                        link(nc.gpsimd.tensor_copy(parts[:, 0, span], x[:]), b, POOL_STEPS)
                        link(nc.gpsimd.tensor_tensor(rest[:], x[:], parts[:, 0, span], ALU.subtract), b, POOL_STEPS)
                        hold()
                        link(nc.gpsimd.tensor_copy(parts[:, 1, span], rest[:]), b, POOL_STEPS)
                        last = nc.gpsimd.tensor_tensor(parts[:, 2, span], rest[:], parts[:, 1, span], ALU.subtract)
                    last.then_inc(parts_ready, 1)
                for u, unit in enumerate(UNITS):
                    if not unit["diag"]:
                        continue
                    pool.wait_ge(scores_read, b * NS + unit["subs"][-1] + 1 + 2)
                    pr = probs[:, u % PROBS, :, 0:P]
                    hold()
                    nc.gpsimd.affine_select(out=pr, in_=pr, pattern=[[0, GH], [1, P]], compare_op=ALU.is_ge,
                                            fill=0.0, base=0, channel_multiplier=-1).then_inc(probs_masked, 1)
                assert steps[0] - base == POOL_STEPS, steps[0] - base

        @block.scalar
        def _(act):
            act.wait_ge(w_loaded, 16 * len(W_DMAS))
            act.sem_inc(scores_read, 2)
            nc.scalar.activation(lam[:], log_lam[:], ACT.Exp, scale=-1.0).then_inc(exp_neg, 1)
            act.wait_ge(w_scaled, 1)
            with act.Fori(0, B) as b:
                for c in range(NC):
                    U = uses_a(b, c)
                    for k in range(SH):
                        act.wait_ge(misc_full[k], U + 1)
                        nc.scalar.activation(drive[:, k, :], M[k][:], ACT.Copy,
                                             scale=one_minus_lam[:, k:k + 1]).then_inc(misc_read[k], 1)
                    act.wait_ge(misc_full[1], U + 2)
                    nc.scalar.activation(x1T[:], M[1][:], ACT.Copy).then_inc(misc_read[1], 1)
                    act.wait_ge(parts_ready, b * NC + c)
                    act.wait_ge(misc_full[0], U + 4)
                    nc.scalar.activation(q_scaled[:], M[0][:], ACT.Copy, scale=qn_col[:]).then_inc(misc_read[0], 1)
                    act.wait_ge(misc_full[1], U + 4)
                    nc.scalar.activation(k_scaled[:], M[1][0:KW, :], ACT.Copy,
                                         scale=kn_col[:]).then_inc(misc_read[1], 1)
                for n, (u, hs) in enumerate(SUBS):
                    w = UNITS[u]["w"]
                    act.wait_ge(scores_ready, b * NS + n + 1)
                    if n == UNITS[u]["subs"][0]:
                        act.wait_ge(probs_used, b * NU + u + 1)
                    dst = probs[:, u % PROBS, hs[0]:hs[-1] + 1, 0:w]
                    two = S2[n % 2]
                    if w > CH // 2:
                        src = two[:, :, 0:w]
                    elif w == CH // 2:
                        src = two[:, :, :].rearrange("p a (h w) -> p (a h) w", w=w)
                    else:
                        src = two[:, 0, :].rearrange("p (h w) -> p h w", w=w)
                    nc.scalar.activation(dst, src, ACT.Exp, bias=shift[:], scale=float(HD) ** -0.5).then_inc(scores_read, 1)
                for c in range(NC):
                    U = uses_c(b, c)
                    act.wait_ge(gate_ready, b * NC + c + 1)
                    g = gate[:].rearrange("p q h d -> p (q h d)")
                    nc.scalar.activation(g, g, ACT.Exp, scale=-1.0).then_inc(gate_exp, 1)
                    act.wait_ge(misc_full[0], U + 3)
                    nc.scalar.activation(ogT[:], M[0][:], ACT.Copy).then_inc(misc_read[0], 1)
                    act.wait_ge(h2T_kept, b * (16 * NC) + 16 * c)
                    act.wait_ge(misc_full[0], U + 4)
                    nc.scalar.activation(h2T[:], M[0][:], ACT.Copy).then_inc(misc_read[0], 1)
            with act.Fori(0, CHUNKS) as n:
                for e in range(E):
                    for f in range(2):
                        act.wait_ge(up_ready, n * (2 * E) + 2 * e + f + 1)
                        nc.scalar.activation(sig[:, f, :], UP[f][1], ACT.Sigmoid,
                                             bias=b_1[:, e, 2 + f:3 + f]).then_inc(sig_ready, 1)

        @block.vector
        def _(dve):
            v = nc.vector
            state = dict(n=0, b=None, per=0)

            def link(ins):
                ins.then_inc(dve_step, 1)
                state["n"] += 1
                dve.wait_ge(dve_step, state["n"] if state["b"] is None else state["b"] * state["per"] + state["n"])

            def rsqrt(y, x, tmp):
                link(v.tensor_scalar(y.bitcast(I32), x.bitcast(I32), -0.5, RSQRT_MAGIC, ALU.mult, ALU.add))
                for _ in range(4):
                    link(v.scalar_tensor_tensor(tmp, y, -0.5, y, ALU.mult, ALU.mult))
                    link(v.tensor_tensor(tmp, tmp, x, ALU.mult))
                    link(v.scalar_tensor_tensor(y, tmp, 1.5, y, ALU.add, ALU.mult))

            dve.wait_ge(w_loaded, 16 * len(W_DMAS))
            dve.wait_ge(exp_neg, 1)
            dve.sem_inc(o_read, NC)
            v.memset(ones[:], 1.0)
            link(v.tensor_scalar(lam[:], lam[:], 1.0, None, ALU.add))
            link(v.reciprocal(lam[:], lam[:]))
            link(v.tensor_scalar(one_minus_lam[:], lam[:], -1.0, 1.0, ALU.mult, ALU.add))
            link(v.tensor_scalar(d_col[:], d_col[:], 1.0, None, ALU.add))
            v.tensor_scalar(skip_diag[:], idm[:], d_col[:], None, ALU.mult)
            v.tensor_scalar(w_qkv[:], w_qkv[:], ln1_col[:], None, ALU.mult)
            v.tensor_scalar(w_r[:], w_r[:], ln2_col[:], None, ALU.mult)
            w1f = w_1[:].rearrange("p e f -> p (e f)")
            v.tensor_scalar(w1f, w1f, ln2_col[:], None, ALU.mult)
            link(v.tensor_tensor(bound[:], norm_rows[:, 0, :], norm_rows[:, 1, :], ALU.mult))
            link(v.scalar_tensor_tensor(bound[:], bound[:], -1.0, bound[:], ALU.mult, ALU.max))
            link(v.tensor_reduce(shift[:], bound[:], AX_X, ALU.max))
            link(v.tensor_scalar(shift[:], shift[:], -float(HD) ** 0.5, SHIFT_FROM, ALU.mult, ALU.add))
            v.tensor_scalar(shift[:], shift[:], 0.0, None, ALU.min).then_inc(w_scaled, 1)

            base = state["n"]
            with dve.Fori(0, B) as b:
                state.update(n=base, b=b, per=DVE_STEPS)
                for c in range(NC):
                    cc = b * NC + c
                    U = uses_a(b, c)
                    for k in range(SH):
                        dve.wait_ge(misc_read[k], U + 1)
                        v.tensor_tensor_scan(xs[:, c, k, :], lam[:, k:k + 1].to_broadcast([P, CH]), drive[:, k, :],
                                             0.0 if c == 0 else xs[:, c - 1, k, CH - 1:CH],
                                             ALU.mult, ALU.add).then_inc(scan_done, 1)
                    dve.wait_ge(misc_full[0], U + 2)
                    for q in range(TQ):
                        ins = v.bn_stats(stats[:, q, :], M[0][:, P * q:P * q + P])
                    link(ins)
                    dve.sem_inc(dve_held, 1)
                    for q in range(TQ):
                        ins = v.bn_aggr(mv[:, q, :], stats[:, q, :])
                    link(ins)
                    v.tensor_scalar(ln_arg[:, 0:TQ], mv[:, :, 1], LN_EPS, None, ALU.add)
                    link(v.tensor_scalar(ln_arg[:, TQ:], mv[:, :, 1], 1.0 + RMS_EPS, LN_EPS * RMS_EPS, ALU.mult, ALU.add))
                    rsqrt(ln_rs[:], ln_arg[:], ln_tmp[:])
                    dve.wait_ge(x1_kept, cc)
                    for q in range(TQ):
                        ins = v.tensor_scalar(x1[:, q, :], M[0][:, P * q:P * q + P], mv[:, q, 0:1], ln_rs[:, q:q + 1],
                                              ALU.subtract, ALU.mult)
                    ins.then_inc(misc_read[0], 1)
                    link(v.tensor_tensor(r1[:], ln_arg[:, 0:TQ], ln_rs[:, 0:TQ], ALU.mult))
                    link(v.tensor_tensor(r1[:], r1[:], ln_rs[:, TQ:], ALU.mult))
                    for half in range(2):
                        dve.wait_ge(misc_full[half], U + 3)
                        for q in (2 * half, 2 * half + 1):
                            w3 = QW + 2 * KW
                            ins = v.scalar_tensor_tensor(qkv[:, q, :], M[half][:, w3 * (q % 2):w3 * (q % 2) + w3],
                                                         r1[:, q:q + 1], b_qkv[:], ALU.mult, ALU.add)
                        ins.then_inc(misc_read[half], 1)
                    dve.wait_ge(misc_read[1], U + 3)
                    dve.wait_ge(misc_read[0], U + 3)
                    for q in range(TQ):
                        ins = v.tensor_tensor(rot_a[:, q, :].rearrange("p (h d) -> p h d", d=HD),
                                              qkv[:, q, 0:QW + KW].rearrange("p (h d) -> p h d", d=HD),
                                              cos_t[:, TQ * c + q, :].unsqueeze(1).to_broadcast([P, NQ + NKV, HD]), ALU.mult)
                    link(ins)
                    dve.wait_ge(rot_b_ready, cc + 1)
                    link(v.tensor_tensor(rot_a[:], rot_a[:], rot_b[:], ALU.add))
                    link(v.tensor_tensor(rot_b[:], rot_a[:], rot_a[:], ALU.mult))
                    link(v.tensor_reduce(hs_arg[:], rot_b[:].rearrange("p q (h d) -> p (q h) d", d=HD), AX_X, ALU.add))
                    link(v.tensor_scalar(hs_arg[:], hs_arg[:], 1.0 / HD, RMS_EPS, ALU.mult, ALU.add))
                    rsqrt(hs_rs[:], hs_arg[:], hs_tmp[:])
                    rs = hs_rs[:].rearrange("p (q h) -> p q h", q=TQ).unsqueeze(3)
                    ra = rot_a[:].rearrange("p q (h d) -> p q h d", d=HD)
                    v.tensor_tensor(qn[:].rearrange("p q (h d) -> p q h d", d=HD), ra[:, :, 0:NQ, :],
                                    rs[:, :, 0:NQ, :].to_broadcast([P, TQ, NQ, HD]), ALU.mult)
                    v.tensor_tensor(kn[:].rearrange("p q (h d) -> p q h d", d=HD), ra[:, :, NQ:, :],
                                    rs[:, :, NQ:, :].to_broadcast([P, TQ, NKV, HD]), ALU.mult).then_inc(qkn_ready, 1)
                for u, unit in enumerate(UNITS):
                    if unit["last"]:
                        dve.wait_ge(probs_used, b * NU + u + 1 + PROBS)
                        v.tensor_copy(oT[:, unit["g"], CH * unit["c"]:CH * unit["c"] + CH],
                                      O[unit["c"]][:]).then_inc(o_read, 1)
                for c in range(NC):
                    cc = b * NC + c
                    U = uses_c(b, c)
                    for q in range(TQ):
                        m = M[q % 2][:, 0:NKV * RCOLS].rearrange("p (g x) -> p g x", x=RCOLS)
                        heads = m[:, :, 0:GH * RH].rearrange("p g (j y) -> p g j y", y=RH)
                        dve.wait_ge(misc_full[q % 2], U + q // 2 + 1)
                        rd = r_den[:].rearrange("p (g j) -> p g j", j=GH)
                        link(v.reciprocal(rd, m[:, :, GH * RH:]))
                        rd = rd.unsqueeze(3).to_broadcast([P, NKV, GH, HD])
                        v.tensor_tensor(o_n[:, q].rearrange("p (g j) d -> p g j d", j=GH), heads[:, :, :, 0:HD], rd, ALU.mult)
                        v.tensor_tensor(gate[:, q].rearrange("p (g j) d -> p g j d", j=GH), heads[:, :, :, HD:], rd,
                                        ALU.mult).then_inc(misc_read[q % 2], 1)
                        dve.wait_ge(misc_read[q % 2], U + q // 2 + 1)
                    g = gate[:].rearrange("p q h d -> p q (h d)")
                    v.tensor_tensor(g, g, bg_b[:].rearrange("p h d -> p (h d)").unsqueeze(1).to_broadcast([P, TQ, QW]),
                                    ALU.add).then_inc(gate_ready, 1)
                    dve.wait_ge(gate_exp, cc + 1)
                    link(v.tensor_scalar(g, g, 1.0, None, ALU.add))
                    link(v.reciprocal(g, g))
                    v.tensor_tensor(og[:], o_n[:].rearrange("p q h d -> p q (h d)"), g, ALU.mult).then_inc(og_ready, 1)
                    dve.wait_ge(misc_full[1], U + 3)
                    tiles = bass.ds(b * NT + TQ * c, TQ)
                    v.tensor_tensor(x2[:], M[1][:].rearrange("p (q d) -> p q d", d=D), resid[:, tiles, :],
                                    ALU.add).then_inc(misc_read[1], 1)
                    dve.wait_ge(misc_read[1], U + 3)
                    link(v.tensor_tensor(x2[:], x2[:], bo_b[:].unsqueeze(1).to_broadcast([P, TQ, D]), ALU.add))
                    v.tensor_tensor(resid[:, tiles, :], resid[:, tiles, :], x2[:], ALU.add)
                    link(v.tensor_tensor(sq[:], x2[:], x2[:], ALU.mult))
                    link(v.tensor_reduce(r2_arg[:], sq[:], AX_X, ALU.add))
                    link(v.tensor_scalar(r2_arg[:], r2_arg[:], 1.0 / D, RMS_EPS, ALU.mult, ALU.add))
                    rsqrt(r2[:], r2_arg[:], r2_tmp[:])
                    v.tensor_tensor(h2[:], x2[:], r2[:].unsqueeze(2).to_broadcast([P, TQ, D]),
                                    ALU.mult).then_inc(h2_ready, 1)
                    dve.wait_ge(misc_full[1], U + 4)
                    v.tensor_tensor(lg[:], M[1][:, 0:TQ * E].rearrange("p (q e) -> p q e", e=E),
                                    br_b[:].unsqueeze(1).to_broadcast([P, TQ, E]), ALU.add).then_inc(misc_read[1], 1)
                    dve.wait_ge(misc_read[1], U + 4)
                    top = lg_max[:].unsqueeze(2).to_broadcast([P, TQ, E])
                    link(v.tensor_reduce(lg_max[:], lg[:], AX_X, ALU.max))
                    link(v.tensor_tensor(lg[:], lg[:], top, ALU.is_ge))
                    link(v.tensor_tensor(lg[:], lg[:], rank8[:].unsqueeze(1).to_broadcast([P, TQ, E]), ALU.mult))
                    link(v.tensor_reduce(lg_max[:], lg[:], AX_X, ALU.max))
                    link(v.tensor_tensor(onehot[:, tiles, :], lg[:], top, ALU.is_equal))
                assert state["n"] - base == DVE_STEPS, state["n"] - base
            base = base + B * DVE_STEPS
            with dve.Fori(0, CHUNKS) as n:
                state.update(n=base, b=n, per=DVE_STEPS_D)
                oh = onehot[:, bass.ds(n * TQ, TQ), :]
                for e in range(E):
                    for f in range(2):
                        k = 2 * e + f
                        dve.wait_ge(sig_ready, n * (2 * E) + k + 1)
                        v.scalar_tensor_tensor(actT[:, e % 2, f, :], UP[f][0], b_1[:, e, f:f + 1], sig[:, f, :],
                                               ALU.add, ALU.mult).then_inc(act_ready, 1)
                    dve.wait_ge(y_ready, n * E + e + 1)
                    for q in range(TQ):
                        y = Y[:, P * q:P * q + P]
                        if e == 0:
                            ins = v.scalar_tensor_tensor(acc[:, q, :], y, oh[:, q, e:e + 1], resid[:, bass.ds(n * TQ + q, 1), :].squeeze(1),
                                                         ALU.mult, ALU.add)
                        else:
                            ins = v.scalar_tensor_tensor(acc[:, q, :], y, oh[:, q, e:e + 1], acc[:, q, :], ALU.mult, ALU.add)
                    ins.then_inc(y_read, 1)
                    dve.wait_ge(y_read, n * E + e + 1)
                for q in range(TQ):
                    ins = v.bn_stats(stats[:, q, :], acc[:, q, :])
                link(ins)
                dve.sem_inc(dve_held, 1)
                for q in range(TQ):
                    ins = v.bn_aggr(mv[:, q, :], stats[:, q, :])
                link(ins)
                link(v.tensor_scalar(r2_arg[:], mv[:, :, 1], LN_EPS, None, ALU.add))
                rsqrt(r2[:], r2_arg[:], r2_tmp[:])
                dve.wait_ge(stored, n * 16)
                for q in range(TQ):
                    ins = v.tensor_scalar(y_out[:, q, :], acc[:, q, :], mv[:, q, 0:1], r2[:, q:q + 1],
                                          ALU.subtract, ALU.mult)
                ins.then_inc(y_final, 1)
                assert state["n"] - base == DVE_STEPS_D, state["n"] - base

        @block.tensor
        def _(pe):
            mm = nc.tensor.matmul
            pe.wait_ge(w_scaled, 1)
            pe.sem_inc(probs_used, PROBS)
            with pe.Fori(0, B) as b:
                for c in range(NC):
                    cc = b * NC + c
                    U = uses_a(b, c)
                    pe.wait_ge(u_loaded[c], b * 16 + 16)
                    for k in range(SH):
                        pe.wait_ge(misc_read[k], U)
                        mm(M[k][:], w_in[:, P * k:P * k + P], u_sb[:, c, :], start=True, stop=True).then_inc(misc_full[k], 1)
                    pe.wait_ge(scan_done, cc * SH + SH)
                    pe.wait_ge(misc_read[0], U + 1)
                    for q in range(TQ):
                        z = M[0][:, P * q:P * q + P]
                        tok = slice(P * q, P * q + P)
                        for k in range(SH):
                            mm(z, xs[:, c, k, tok], w_out[:, k, :], start=k == 0, stop=False)
                        ins = mm(z, u_sb[:, c, tok], skip_diag[:], start=False, stop=True)
                    ins.then_inc(misc_full[0], 1)
                    pe.wait_ge(misc_read[0], U + 2)
                    pe.wait_ge(misc_read[1], U + 1)
                    for q in range(TQ):
                        ins = nc.tensor.transpose(M[1][:, P * q:P * q + P], x1[:, q, :], idm[:])
                    ins.then_inc(misc_full[1], 1)
                    pe.wait_ge(misc_read[1], U + 2)
                    for q in range(TQ):
                        w3 = QW + 2 * KW
                        ins = mm(M[q // 2][:, w3 * (q % 2):w3 * (q % 2) + w3], x1T[:, P * q:P * q + P], w_qkv[:],
                                 start=True, stop=True)
                        if q % 2:
                            ins.then_inc(misc_full[q // 2], 1)
                    pe.wait_ge(qkn_ready, cc + 1)
                    pe.wait_ge(misc_read[0], U + 3)
                    for q in range(TQ):
                        ins = nc.tensor.transpose(M[0][:, P * q:P * q + P], qn[:, q, :], idm[:])
                    ins.then_inc(misc_full[0], 1)
                    pe.wait_ge(misc_read[1], U + 3)
                    for q in range(TQ):
                        ins = nc.tensor.transpose(M[1][0:KW, P * q:P * q + P], kn[:, q, :], idm[:])
                    ins.then_inc(misc_full[1], 1)

                def score(n):
                    u, hs = SUBS[n]
                    unit = UNITS[u]
                    w, g = unit["w"], unit["g"]
                    t0 = CH * unit["c"] + CH - w
                    key = kT[:, g, P * unit["i"]:P * unit["i"] + P]
                    pe.wait_ge(scores_read, b * NS + n + 1)
                    per_bank = max(1, CH // w)
                    for a in range(0, len(hs), per_bank):
                        k = min(per_bank, len(hs) - a)
                        h0 = GH * g + hs[a]
                        dst = S2[n % 2][:, a // per_bank, 0:k * w]
                        ins = mm(dst, key, qT[:, h0:h0 + k, t0:t0 + w], start=True, stop=True)
                    ins.then_inc(scores_ready, 1)

                def weigh(u):
                    unit = UNITS[u]
                    w, g, c = unit["w"], unit["g"], unit["c"]
                    if unit["first"]:
                        pe.wait_ge(o_read, b * (NKV * NC) + NC * g + c + 1)
                    if unit["diag"]:
                        pe.wait_ge(probs_masked, b * NM + unit["masks_before"] + 1)
                    else:
                        pe.wait_ge(scores_read, b * NS + unit["subs"][-1] + 1 + 2)
                    for j in range(GH):
                        ins = mm(O[c][32 * j:32 * j + 32, CH - w:CH], v_pad[:, unit["i"], g, :], probs[:, u % PROBS, j, 0:w],
                                 start=unit["first"], stop=unit["last"], tile_position=(0, 32 * j))
                    ins.then_inc(probs_used, 1)

                pe.wait_ge(stacked, b * (16 * STACK_DMAS) + 16 * STACK_DMAS)
                pe.wait_ge(v_ready, b * (NC * NKV) + NC * NKV)
                for n in UNITS[0]["subs"]:
                    score(n)
                for u in range(NU + 1):
                    ahead = UNITS[u + 1]["subs"] if u + 1 < NU else []
                    for n in ahead[:1]:
                        score(n)
                    if u >= 1:
                        weigh(u - 1)
                    for n in ahead[1:]:
                        score(n)
                for c in range(NC):
                    cc = b * NC + c
                    U = uses_c(b, c)
                    pe.wait_ge(o_read, b * (NKV * NC) + NKV * NC + 2)
                    for q in range(TQ):
                        pe.wait_ge(misc_read[q % 2], U + q // 2)
                        for g in range(NKV):
                            t = CH * c + P * q
                            ins = mm(M[q % 2][:, RCOLS * g:RCOLS * g + RCOLS], oT[:, g, t:t + P], mix[:], start=True, stop=True)
                        ins.then_inc(misc_full[q % 2], 1)
                    pe.wait_ge(og_ready, cc + 1)
                    pe.wait_ge(misc_read[0], U + 2)
                    for q in range(TQ):
                        ins = nc.tensor.transpose(M[0][:, P * q:P * q + P], og[:, q, :], idm[:])
                    ins.then_inc(misc_full[0], 1)
                    pe.wait_ge(misc_read[0], U + 3)
                    pe.wait_ge(misc_read[1], U + 2)
                    for q in range(TQ):
                        ins = mm(M[1][:, P * q:P * q + P], ogT[:, P * q:P * q + P], w_o[:], start=True, stop=True)
                    ins.then_inc(misc_full[1], 1)
                    pe.wait_ge(h2_ready, cc + 1)
                    for q in range(TQ):
                        ins = nc.tensor.transpose(M[0][:, P * q:P * q + P], h2[:, q, :], idm[:])
                    ins.then_inc(misc_full[0], 1)
                    pe.wait_ge(misc_read[0], U + 4)
                    pe.wait_ge(misc_read[1], U + 3)
                    for q in range(TQ):
                        ins = mm(M[1][:, E * q:E * q + E], h2T[:, P * q:P * q + P], w_r[:], start=True, stop=True)
                    ins.then_inc(misc_full[1], 1)
            pe.wait_ge(misc_read[1], uses_c(B - 1, NC - 1) + 4)
            with pe.Fori(0, CHUNKS) as n:
                tok = tokT[:]
                pe.wait_ge(tok_loaded, n * 16 + 16)

                def down(e):
                    pe.wait_ge(act_ready, n * (2 * E) + 2 * e + 2)
                    pe.wait_ge(y_read, n * E + e)
                    for q in range(TQ):
                        y = Y[:, P * q:P * q + P]
                        mm(y, ones[:], b_2[:, e, :], start=True, stop=False)
                        for f in range(2):
                            ins = mm(y, actT[:, e % 2, f, P * q:P * q + P], w_2[:, e, f, :], start=False, stop=f == 1)
                    ins.then_inc(y_ready, 1)

                for e in range(E):
                    for f in range(2):
                        pe.wait_ge(act_ready, n * (2 * E) + max(0, 2 * e + f - 1))
                        mm(UP[f][0], w_1[:, e, P * f:P * f + P], tok, start=True, stop=True)
                        mm(UP[f][1], w_1[:, e, P * (2 + f):P * (3 + f)], tok, start=True, stop=True).then_inc(up_ready, 1)
                    if e:
                        down(e - 1)
                down(E - 1)


POOL_STEPS = 12
DVE_STEPS = 128
DVE_STEPS_D = 16

_ORDER = ["uT", "WinT", "log_lambda", "WoutT", "Dvec", "ln1_w", "ln2_w", "Wq", "bq", "Wk", "bk", "Wv", "bv", "qn_w",
          "kn_w", "gate_mix", "bg", "Wo", "bo", "Wr", "br", "W1", "b1", "W2", "b2", "ident", "cos8", "sin8", "first_of"]


def shape_constants():
    inv_freq = (np.float32(1.0) / np.float32(10000.0) ** (np.arange(0, HD, 2, dtype=np.float32) / np.float32(HD))).astype(np.float32)
    ang = np.arange(T, dtype=np.float32)[:, None] * inv_freq[None, :]
    c, s = np.cos(ang).astype(np.float32), np.sin(ang).astype(np.float32)
    tiled = lambda a: np.ascontiguousarray(a.reshape(NT, P, HD).transpose(1, 0, 2))
    return {"ident": np.eye(P, dtype=np.float32), "cos8": tiled(np.concatenate([c, c], 1)),
            "sin8": tiled(np.concatenate([-s, s], 1)), "first_of": np.arange(E, 0, -1).astype(np.float32)}


def kernel(**inputs):
    import concourse.bacc as bacc
    from concourse.bass_utils import run_bass_kernel_spmd

    a = {k.replace("L0_attn_", "").replace("L0_ffn_", ""): np.asarray(x) for k, x in inputs.items()}
    gate_mix = np.zeros((P, RCOLS), np.float32)
    for j in range(GH):
        gate_mix[32 * j:32 * j + HD, RH * j:RH * j + HD] = np.eye(HD, dtype=np.float32)
        gate_mix[32 * j:32 * j + HD, RH * j + HD:RH * j + RH] = a["Wg"]
        gate_mix[32 * j + HD, GH * RH + j] = 1.0
    arrays = {"uT": a["u"].transpose(0, 2, 1), "WinT": a["W_in"].T, "WoutT": a["W_out"].T, "Dvec": a["D"],
              "gate_mix": gate_mix, **shape_constants()}
    for name in _ORDER:
        if name not in arrays:
            arrays[name] = a[name]
    nc = bacc.Bacc("TRN2", target_bir_lowering=False, num_devices=1)
    feed, args = {}, []
    for name in _ORDER:
        x = np.ascontiguousarray(arrays[name])
        feed[f"in_{name}"] = x
        args.append(nc.dram_tensor(f"in_{name}", x.shape, mybir.dt.from_np(x.dtype), kind="ExternalInput").ap())
    out = nc.dram_tensor("out", (CHUNKS, P, TQ, D), F32, kind="ExternalOutput").ap()
    block_kernel(nc, *args, out)
    r = run_bass_kernel_spmd(nc, [feed], core_ids=[0])
    got = np.asarray(r.results[0]["out"])
    return got.transpose(0, 2, 1, 3).reshape(B, T, D)
```

```python
from contextlib import ExitStack

import numpy as np

import concourse.bass as bass
from concourse import mybir

F32 = mybir.dt.float32
BF16 = mybir.dt.bfloat16
I32 = mybir.dt.int32
ALU = mybir.AluOpType
ACT = mybir.ActivationFunctionType
AX_X = mybir.AxisListType.X

P = 128
B, T, D = 4, 1024, 128
STATE = 256
SH = STATE // P
NQ, NKV, HD = 16, 4, 8
GH = NQ // NKV
QW, KW = NQ * HD, NKV * HD
HID, E = 256, 8
LN_EPS, RMS_EPS = 1e-5, 1e-6
CH = 512
NC = T // CH
TQ = CH // P
NT = T // P
CHUNKS = B * NC
RSQRT_MAGIC = float(0x5F3759DF)
SHIFT_FROM = 60.0

PARTS = 3
TERMS = PARTS * PARTS

RH = 2 * HD
RCOLS = GH * RH + GH

TOKENS = B * T
REGION = TOKENS + P
SPARE = E * REGION
FULL = TOKENS // P
TILES = TOKENS // P + E
RING = 4
BIAS = 2 * HID + D
assert TILES % RING == 0
SPARE_BASE = SPARE - FULL * P
ROWS = SPARE_BASE + (TILES + 1) * P
ENTRIES = TILES + 1


def attention_units():
    units, subs = [], []
    for c in range(NC):
        for g in range(NKV):
            last = TQ * (c + 1) - 1
            for i in range(last + 1):
                width = CH - P * max(0, i - TQ * c)
                unit = dict(g=g, c=c, i=i, w=width, diag=i >= TQ * c, first=i == 0, last=i == last, subs=[],
                            out=c * NKV + g)
                heads = [(0, 1), (2, 3)] if width > CH // 2 else [(0, 1, 2, 3)]
                for hs in heads:
                    unit["subs"].append(len(subs))
                    subs.append((len(units), hs))
                units.append(unit)
    n = 0
    for u in units:
        u["masks_before"] = n
        n += u["diag"]
    return units, subs


UNITS, SUBS = attention_units()
NU, NS, NM = len(UNITS), len(SUBS), sum(u["diag"] for u in UNITS)
NO = NC * NKV
LAST = {(u["c"], u["g"]): n for n, u in enumerate(UNITS) if u["last"]}
PROBS = 3
assert NU % PROBS == 0 and NS % 2 == 0 and NO % 2 == 0

RUNS = {"A0": (1, 0), "A1": (1, 1), "C1": (-1, 1), "C0": (0, 0)}
BANKLESS = ("gate", "scatter0", "scatter1", "scatter2", "scatter3")
AT_A = dict(up0=0, up1=1, z=12, x1T=34, qkv01=38, qkv23=39, qT=66, kT=68)
AT_C = dict(row0=5, row1=7, row2=9, row3=11, gate=35, ogT=37, proj=45, h2T=83, logits=87, rank=94, scatter0=97, scatter1=98, scatter2=98.5, scatter3=99)


def unit_time(unit):
    return len(unit["subs"]) * 0.19 + GH * unit["w"] * 0.833e-3


def plan(first_half, second_half):
    total, now = sum(unit_time(u) for u in UNITS), 0.0
    start = []
    for unit in UNITS:
        start.append(now / total * 200)
        now += unit_time(unit)
    pieces = []
    for half, runs in enumerate((first_half, second_half)):
        for run in runs:
            at = AT_A if run[0] == "A" else AT_C
            pieces += [(100 * half + t, run, name) for name, t in at.items()]
    pieces.sort(key=lambda x: x[0])
    steps, u = [[] for _ in UNITS], 0
    for t, run, name in pieces:
        while u + 1 < NU and (start[u] < t or sum(n not in BANKLESS for _, n in steps[u]) >= 2
                              or (run[0] == "C" and any(r == run for r, _ in steps[u]) and u < NU - 1)):
            u += 1
        steps[u].append((run, name))
    return steps


PLANS = {"first": plan(("A0",), ("A1", "C0")), "steady": plan(("A0", "C1"), ("A1", "C0")), "last": plan(("C1",), ("C0",))}
PRO = [("A0", n) for n in ("up0", "up1")] + [("A1", n) for n in ("up0", "up1")] + [("A0", n) for n in ("z", "x1T")] \
    + [("A1", "z")] + [("A0", n) for n in ("qkv01", "qkv23")] + [("A1", "x1T")] + [("A0", n) for n in ("qT", "kT")] \
    + [("A1", n) for n in ("qkv01", "qkv23", "qT", "kT")]
EPI = [("C1", n) for n in AT_C]


def number(pieces):
    return {p: j for j, p in enumerate([p for p in pieces if p[1] not in BANKLESS])}


FILLS = {"before": number(PRO), "after": number(EPI), **{k: number(sum(v, [])) for k, v in PLANS.items()}}
N_FIRST = len(FILLS["before"])
N_STEADY = len(FILLS["steady"])
N_OFF = N_FIRST + len(FILLS["first"]) - N_STEADY
assert N_STEADY % 2 == 0


def fillings(kind, b, run):
    where = {}
    for (r, name), j in FILLS[kind].items():
        if r != run:
            continue
        if kind in ("before", "first"):
            n = j + (N_FIRST if kind == "first" else 0)
            where[name] = n % 2, n // 2
        else:
            j += N_OFF
            if kind == "after":
                j -= N_STEADY - len(FILLS["last"])
            where[name] = j % 2, b * (N_STEADY // 2) + j // 2
    return where


def block_kernel(nc, uT, WinT, log_lambda, WoutT, Dvec, ln1_w, ln2_w, Wq, bq, Wk, bk, Wv, bv, qn_w, kn_w,
                 gate_mix, bg, Wo, bo, Wr, br, W1, b1, W2, b2, ident, cos8, sin8, first_of,
                 all_ones, earlier, regions, tile_nos, expert_nos, out):
    with ExitStack() as ctx:
        def sb(name, shape, dt=F32):
            return ctx.enter_context(nc.sbuf_tensor(name, shape, dt))

        def sem(name):
            return ctx.enter_context(nc.semaphore(name))

        w_in = sb("w_in", [P, STATE])
        w_out = sb("w_out", [P, SH, D])
        log_lam = sb("log_lam", [P, SH])
        lam = sb("lam", [P, SH])
        one_minus_lam = sb("one_minus_lam", [P, SH])
        d_col = sb("d_col", [P, 1])
        skip_diag = sb("skip_diag", [P, P])
        idm = sb("idm", [P, P])
        ln1_col = sb("ln1_col", [P, 1])
        ln2_col = sb("ln2_col", [P, 1])
        w_qkv = sb("w_qkv", [P, QW + 2 * KW])
        b_qkv = sb("b_qkv", [P, QW + 2 * KW])
        qn_col = sb("qn_col", [P, 1])
        kn_col = sb("kn_col", [KW, 1])
        norm_rows = sb("norm_rows", [P, 2, HD])
        bound = sb("bound", [P, HD])
        shift = sb("shift", [P, 1])
        mix = sb("mix", [P, RCOLS])
        bg_b = sb("bg_b", [P, NQ, HD])
        w_o = sb("w_o", [P, D])
        bo_b = sb("bo_b", [P, D])
        w_r = sb("w_r", [P, E])
        br_b = sb("br_b", [P, E])
        rank8 = sb("rank8", [P, E])
        w_1 = sb("w_1", [P, E, 2 * HID])
        bias = sb("bias", [PARTS, E, BIAS], BF16)
        ones_bf = sb("ones_bf", [PARTS, P], BF16)
        zero_rows = sb("zero_rows", [P, D])
        ones_sq = sb("ones_sq", [P, P])
        before = sb("before", [P, P])
        region_of = sb("region_of", [P, E])
        tile_no = sb("tile_no", [1, ENTRIES])
        tile_steps = sb("tile_steps", [P, FULL])
        expert_no = sb("expert_no", [1, E])
        w_2 = sb("w_2", [P, E, 2, D])
        cos_t = sb("cos_t", [P, NT, HD])
        sin_t = sb("sin_t", [P, NT, HD])

        u_sb = sb("u_sb", [P, NC, CH])
        xs = sb("xs", [P, NC, SH, CH])
        stats = sb("stats", [P, TQ, 6])
        mv = sb("mv", [P, TQ, 2])
        ln_arg = sb("ln_arg", [P, 2 * TQ])
        ln_rs = sb("ln_rs", [P, 2 * TQ])
        ln_tmp = sb("ln_tmp", [P, 2 * TQ])
        r1 = sb("r1", [P, TQ])
        x1 = sb("x1", [P, TQ, D])
        x1T = sb("x1T", [P, CH])
        qkv = sb("qkv", [P, TQ, QW + 2 * KW])
        rot_a = sb("rot_a", [P, TQ, QW + KW])
        rot_b = sb("rot_b", [P, TQ, QW + KW])
        hs_arg = sb("hs_arg", [P, TQ * (NQ + NKV)])
        hs_rs = sb("hs_rs", [P, TQ * (NQ + NKV)])
        hs_tmp = sb("hs_tmp", [P, TQ * (NQ + NKV)])
        qn = sb("qn", [P, TQ, QW])
        kn = sb("kn", [P, TQ, KW])
        q_scaled = sb("q_scaled", [P, CH])
        k_scaled = sb("k_scaled", [KW, CH])
        v_next = sb("v_next", [P, NT, KW])
        q_parts = sb("q_parts", [P, PARTS, T], BF16)
        k_parts = sb("k_parts", [KW, PARTS, T], BF16)
        resid = sb("resid", [P, B * NT, D])

        q_spill = nc.dram_tensor("q_spill", (NC, PARTS, HD, NQ, CH), BF16, kind="Internal").ap()
        k_spill = nc.dram_tensor("k_spill", (NC, NKV, PARTS, HD, CH), BF16, kind="Internal").ap()

        qT = sb("qT", [P, NC, NQ, CH], BF16)
        kT = sb("kT", [P, NKV, T], BF16)
        v_pad = sb("v_pad", [P, NT, NKV, 32])
        probs = sb("probs", [P, PROBS, GH, CH])
        oT = sb("oT", [P, NKV, T])
        early = probs[0:E].rearrange("e n j t -> e (n j t)")
        bias_in, bias_rest = early[:, 0:BIAS], early[:, BIAS:2 * BIAS]
        bias_split = early[:, 2 * BIAS:2 * BIAS + PARTS * BIAS // 2].bitcast(BF16).rearrange("e (p x) -> e p x", p=PARTS)

        r_den = sb("r_den", [P, TQ, NQ])
        o_n = sb("o_n", [P, TQ, NQ, HD])
        gate = sb("gate", [P, TQ, NQ, HD])
        og = sb("og", [P, TQ, QW])
        ogT = sb("ogT", [P, CH])
        x2 = sb("x2", [P, TQ, D])
        sq = og
        r2_arg = sb("r2_arg", [P, TQ])
        r2 = sb("r2", [P, TQ])
        r2_tmp = sb("r2_tmp", [P, TQ])
        h2 = sb("h2", [P, TQ, D])
        h2T = sb("h2T", [P, CH])
        lg = sb("lg", [P, TQ, E])
        lg_max = sb("lg_max", [P, TQ])
        onehot = sb("onehot", [P, TQ, E])
        no_tokens = sb("no_tokens", [P, E])
        seen = sb("seen", [P, TQ + 1, E])
        slot_f = sb("slot_f", [P, TQ, E])
        slot_s = sb("slot_s", [P, TQ])
        slot = sb("slot", [P, TQ], I32)
        slots = sb("slots", [P, B * NT])
        xs_rows = nc.dram_tensor("xs_rows", (ROWS, D), F32, kind="Internal").ap()
        ys_rows = nc.dram_tensor("ys_rows", (TILES * P, D), F32, kind="Internal").ap()

        count = sb("count", [P, E])
        n_tiles = sb("n_tiles", [P, E])
        end_tile = sb("end_tile", [P, E])
        start_tile = sb("start_tile", [P, E])
        packed_off = sb("packed_off", [P, E])
        packed_step = sb("packed_step", [P, E])
        region_a = sb("region_a", [P, E])
        row_f = sb("row_f", [1, ENTRIES])
        exp_f = sb("exp_f", [1, ENTRIES])
        tile_row = sb("tile_row", [1, ENTRIES], I32)
        tile_expert = sb("tile_expert", [1, ENTRIES], I32)
        fill_row = sb("fill_row", [1, E], I32)
        carve = oT[:].rearrange("p g t -> p (g t)")
        slot_ge = carve[:, 2816:3072].rearrange("p (t e) -> p t e", e=E)
        over = carve[:, 2816:3072].rearrange("p (e n) -> p e n", e=E)
        mine = carve[0:1, 3072:3072 + ENTRIES * E].rearrange("p (k e) -> p k e", e=E)
        mine_x = carve[0:1, 3584:3584 + ENTRIES * E].rearrange("p (k e) -> p k e", e=E)
        x_in = carve[:, 0:512].rearrange("p (n d) -> p n d", d=D)
        y_sb = carve[:, 512:1024].rearrange("p (n d) -> p n d", d=D)
        xT = carve[:, 1024:1280].rearrange("p (n d) -> p n d", d=D)
        sig = carve[:, 1280:1792].rearrange("p (n d) -> p n d", d=HID)
        hid = carve[:, 1792:2304].rearrange("p (n d) -> p n d", d=HID)
        hidT = carve[:, 2304:2816].rearrange("p (n d) -> p n d", d=HID)

        y_tok = probs[:, 0, 0:2, :]
        z2 = probs[:, 0, 2:4, :]
        y_out = probs[:, 1, 0:2, :]
        moved = sb("moved", [P, B * NT])
        packed = sb("packed", [P, B * NT], I32)
        index = sb("index", [P, 2, TQ], I32)

        S2 = [ctx.enter_context(nc.psum_tensor(f"scores{i}", [P, 2, CH], F32)) for i in range(2)]
        O = [ctx.enter_context(nc.psum_tensor(f"outputs{i}", [P, CH], F32)) for i in range(2)]
        M = [ctx.enter_context(nc.psum_tensor(f"misc{i}", [P, CH], F32)) for i in range(2)]
        PX, PU, PH, PY = M, [S2[0][:, i, :] for i in range(2)], [S2[1][:, i, :] for i in range(2)], O

        w_loaded = sem("w_loaded")
        u_loaded = [sem(f"u_loaded{c}") for c in range(NC)]
        late_loaded = sem("late_loaded")
        w_scaled = sem("w_scaled")
        late_ready = sem("late_ready")
        zeroed = sem("zeroed")
        misc_full = [sem(f"misc_full{i}") for i in range(2)]
        misc_read = [sem(f"misc_read{i}") for i in range(2)]
        scan_done = sem("scan_done")
        dve_step = sem("dve_step")
        pool_step = sem("pool_step")
        pool_held = sem("pool_held")
        dve_held = sem("dve_held")
        sp_held = sem("sp_held")
        qkn_ready = sem("qkn_ready")
        x1_kept = sem("x1_kept")
        parts_ready = sem("parts_ready")
        x2_kept = sem("x2_kept")
        v_kept = sem("v_kept")
        v_copied = sem("v_copied")
        spilled = [sem(f"spilled{c}") for c in range(NC)]
        stacked = [[sem(f"stacked{c}_{g}") for g in range(NKV)] for c in range(NC)]
        scores_ready = sem("scores_ready")
        scores_read = sem("scores_read")
        probs_masked = sem("probs_masked")
        probs_used = sem("probs_used")
        o_read = sem("o_read")
        gate_ready = sem("gate_ready")
        gate_tanh = sem("gate_tanh")
        og_ready = sem("og_ready")
        h2_ready = sem("h2_ready")
        exp_neg = sem("exp_neg")
        bias_split_ready = sem("bias_split_ready")
        bias_ready = sem("bias_ready")
        route_ready = sem("route_ready")
        slot_ready = sem("slot_ready")
        slots_kept = sem("slots_kept")
        scattered = sem("scattered")
        count_ready = sem("count_ready")
        table_ready = sem("table_ready")
        filled = sem("filled")
        packed_ready = sem("packed_ready")
        x_loaded = [sem(f"x_loaded{i}") for i in range(RING)]
        x_turned = sem("x_turned")
        xT_ready = sem("xT_ready")
        up_ready = sem("up_ready")
        sig_ready = sem("sig_ready")
        hid_ready = sem("hid_ready")
        hid_turned = sem("hid_turned")
        hidT_ready = sem("hidT_ready")
        y_ready = sem("y_ready")
        y_copied = sem("y_copied")
        y_kept = [sem(f"y_kept{i}") for i in range(RING)]
        gathered = [sem(f"gathered{i}") for i in range(2)]
        y_tok_read = sem("y_tok_read")
        y_final = sem("y_final")
        stored = [sem(f"stored{i}") for i in range(2)]

        def filled_bank(eng, place):
            eng.wait_ge(misc_full[place[0]], place[1] + 1)

        def read_bank(eng, place):
            eng.wait_ge(misc_read[place[0]], place[1] + 1)

        def free_bank(eng, place):
            eng.wait_ge(misc_read[place[0]], place[1])

        def need(eng, sem, n):
            if not (isinstance(n, int) and n <= 0):
                eng.wait_ge(sem, n)

        def over_tiles(eng, step):
            for j in range(RING):
                step(j, j, 0)
            with eng.Fori(1, TILES // RING) as it:
                for j in range(RING):
                    step(it * RING + j, j, it)

        row = lambda ap, n: ap.rearrange("(a n) -> a n", a=1).to_broadcast([n, ap.shape[0]])
        col = lambda ap: ap.rearrange("(p a) -> p a", a=1)

        every = lambda ap, n, m: ap.rearrange("(a b d) -> a b d", a=1, b=1).to_broadcast([n, m, ap.shape[0]])
        heads_col = lambda ap, n: ap.rearrange("(h d a) -> h d a", h=1, a=1).to_broadcast([n, HD, 1])
        EARLY = [
            (w_in[:], WinT), (log_lam[:], log_lambda.rearrange("(k p) -> p k", p=P)), (d_col[:], col(Dvec)),
            (idm[:], ident), (w_out[:], WoutT.rearrange("(k p) d -> p k d", p=P)), (ln1_col[:], col(ln1_w)),
            (w_qkv[:, 0:QW], Wq), (w_qkv[:, QW:QW + KW], Wk), (w_qkv[:, QW + KW:], Wv),
            (b_qkv[:, 0:QW], row(bq, P)), (b_qkv[:, QW:QW + KW], row(bk, P)), (b_qkv[:, QW + KW:], row(bv, P)),
            (cos_t[:], cos8), (sin_t[:], sin8), (qn_col[:], heads_col(qn_w, NQ)), (kn_col[:], heads_col(kn_w, NKV)),
        ]
        LATE = [
            (bias_in[:, 0:2 * HID], b1), (bias_in[:, 2 * HID:], b2), (ln2_col[:], col(ln2_w)),
            (norm_rows[:, 0, :], row(qn_w, P)), (norm_rows[:, 1, :], row(kn_w, P)),
            (mix[:], gate_mix), (w_o[:], Wo), (bo_b[:], row(bo, P)), (w_r[:], Wr), (br_b[:], row(br, P)),
            (rank8[:], row(first_of, P)), (w_1[:], W1.rearrange("e p f -> p e f")),
            (w_2[:], W2.rearrange("e (k p) d -> p e k d", p=P)), (ones_sq[:], all_ones), (before[:], earlier),
            (region_of[:], row(regions, P)), (tile_no[:], row(tile_nos, 1)), (tile_steps[:], row(tile_nos[0:FULL], P)),
            (expert_no[:], row(expert_nos, 1)), (bg_b[:], every(bg, P, NQ)),
        ]

        block = ctx.enter_context(nc.Block())

        SPILL = 16 * 2 * PARTS
        STACK = 16 * (PARTS + 1)

        @block.sync
        def _(sp):
            def load_u(b, c, later=0):
                sp.dma_start(u_sb[:, c, :], uT[later:][b, :, CH * c:CH * c + CH]).then_inc(u_loaded[c], 16)

            def spill(b, c, later=0):
                span = slice(CH * c, CH * c + CH)
                for g in range(NKV):
                    sp.wait_ge(stacked[c][g], b * STACK + later * STACK)
                sp.wait_ge(parts_ready, b * NC + (later * NC + c + 1))
                for p in range(PARTS):
                    sp.dma_start(q_spill[c, p].rearrange("d h t -> h d t"), q_parts[:, p, span]).then_inc(spilled[c], 16)
                for p in range(PARTS):
                    sp.dma_start(k_spill[c, :, p], k_parts[:, p, span]).then_inc(spilled[c], 16)

            def stack(b, c, g, later=0):
                span = slice(CH * c, CH * c + CH)
                if later:
                    sp.wait_ge(scores_ready, b * NS + (UNITS[LAST[NC - 1, g]]["subs"][-1] + 1))
                sp.wait_ge(spilled[c], b * SPILL + (later * SPILL + SPILL))
                for p in range(PARTS):
                    src = q_spill[c, p:p + 1, :, GH * g:GH * g + GH, :].rearrange("a d h t -> a d (h t)")
                    sp.dma_start(qT[HD * PARTS * p:HD * PARTS * (p + 1), c, GH * g:GH * g + GH, :],
                                 src.to_broadcast([PARTS, HD, GH * CH])).then_inc(stacked[c][g], 16)
                src = k_spill[c, g:g + 1].rearrange("a p d t -> a (p d) t")
                sp.dma_start(kT[0:HD * TERMS, g, span], src.to_broadcast([PARTS, PARTS * HD, CH])).then_inc(stacked[c][g], 16)

            def body(b, prefetch):
                if prefetch:
                    sp.wait_ge(x1_kept, b * NC + 3)
                    sp.sem_inc(sp_held, 1)
                    load_u(b, 0, 2)
                spill(b, 0, 1)
                stack(b, 0, 0, 1)
                if prefetch:
                    sp.wait_ge(x1_kept, b * NC + 4)
                    sp.sem_inc(sp_held, 1)
                    load_u(b, 1, 2)
                stack(b, 0, 1, 1)
                stack(b, 0, 2, 1)
                spill(b, 1, 1)
                stack(b, 0, 3, 1)
                for g in range(NKV):
                    stack(b, 1, g, 1)

            for c in range(NC):
                load_u(0, c)
            for dst, src in EARLY:
                sp.dma_start(dst, src, allow_slow_non_contiguous=True).then_inc(w_loaded, 16)
            for c in range(NC):
                sp.wait_ge(x1_kept, c + 1)
                load_u(1, c)
            sp.wait_ge(zeroed, 1)
            for c in range(NC):
                spill(0, c)
                for g in range(NKV):
                    stack(0, c, g)
            with sp.Fori(0, B - 2) as b:
                body(b, True)
            body(B - 2, False)
            sp.wait_ge(table_ready, 1)
            for e in range(E):
                r = sp.value_load(fill_row[0:1, e:e + 1], min_val=0, max_val=ROWS - P)
                sp.dma_start(xs_rows[bass.ds(r, P), :], zero_rows[:]).then_inc(filled, 16)
            spare = xs_rows[SPARE:ROWS, :].rearrange("(n p) d -> p n d", p=P)
            sp.dma_start(spare, zero_rows[:].unsqueeze(1).to_broadcast([P, ENTRIES - FULL, D])).then_inc(filled, 16)
            sp.wait_ge(scattered, 16 * B * NT)
            sp.wait_ge(filled, 16 * (E + 1))

            def load(k, j, it):
                need(sp, x_turned, k - RING + 1)
                r = sp.value_load(tile_row[0:1, bass.ds(k, 1)], min_val=0, max_val=ROWS - P)
                sp.dma_start(x_in[:, j, :], xs_rows[bass.ds(r, P), :]).then_inc(x_loaded[j], 16)
            over_tiles(sp, load)
            load(TILES, 0, TILES // RING)
            with sp.Fori(0, CHUNKS // 2) as m:
                for j in range(2):
                    sp.wait_ge(y_final, m * 2 + j + 1)
                    sp.dma_start(out[bass.ds(m * 2 + j, 1)].rearrange("a p q d -> (a p) (q d)"), y_out[:, j, :]).then_inc(stored[j], 16)
            for j in range(2):
                sp.wait_ge(stored[j], 16 * CHUNKS // 2 + 16)

        @block.gpsimd
        def _(pool):
            state = dict(n=0, b=None, per=0)

            def link(ins):
                ins.then_inc(pool_step, 1)
                state["n"] += 1
                pool.wait_ge(pool_step, state["n"] if state["b"] is None else state["b"] * state["per"] + state["n"])

            def hold():
                pool.sem_inc(pool_held, 1)

            def piece(kind, at, run, name):
                L = fillings(kind, at, run)
                b, c = at + RUNS[run][0], RUNS[run][1]
                cc = b * NC + c
                span = slice(CH * c, CH * c + CH)
                if name == "qkv23":
                    read_bank(pool, L["qkv01"])
                    read_bank(pool, L["qkv23"])
                    pool.wait_ge(v_copied, b * NKV)
                    hold()
                    nc.gpsimd.tensor_copy(v_next[:, TQ * c:TQ * c + TQ, :], qkv[:, :, QW + KW:]).then_inc(v_kept, 1)
                elif name == "h2T":
                    pool.wait_ge(h2_ready, cc + 1)
                    hold()
                    tiles = resid[:, bass.ds(b * NT + TQ * c, TQ), :]
                    nc.gpsimd.tensor_tensor(tiles, tiles, x2[:], ALU.add).then_inc(x2_kept, 1)
                elif name.startswith("scatter"):
                    q = int(name[-1])
                    if q == 0:
                        pool.wait_ge(slot_ready, cc + 1)
                        hold()
                        nc.gpsimd.tensor_copy(slots[:, bass.ds(b * NT + TQ * c, TQ)], slot[:]).then_inc(slots_kept, 1)
                    nc.gpsimd.indirect_dma_start(
                        xs_rows, bass.IndirectOffsetOnAxis(ap=slot[:, q:q + 1], axis=0),
                        h2[:, q, :], None).then_inc(scattered, 16)

            def copy_v(b, g):
                pool.wait_ge(v_kept, b * NC + NC)
                if not (isinstance(b, int) and b == 0):
                    pool.wait_ge(probs_used, (b - 1) * NU + LAST[NC - 1, g] + 1 + PROBS)
                hold()
                nc.gpsimd.tensor_copy(v_pad[:, :, g, 0:HD], v_next[:, :, HD * g:HD * g + HD]).then_inc(v_copied, 1)

            def mask(b, u):
                if not UNITS[u]["diag"]:
                    return
                pool.wait_ge(scores_read, b * NS + UNITS[u]["subs"][-1] + 1 + 2)
                pr = probs[:, u % PROBS, :, 0:P]
                hold()
                nc.gpsimd.affine_select(out=pr, in_=pr, pattern=[[0, GH], [1, P]], compare_op=ALU.is_ge,
                                        fill=0.0, base=0, channel_multiplier=-1).then_inc(probs_masked, 1)

            def body(kind, b):
                for u in range(NU):
                    if u + 1 < NU:
                        mask(b, u + 1)
                    elif kind != "last":
                        mask(b + 1, 0)
                    if u == 2 and kind != "first":
                        copy_v(b, NKV - 1)
                    if u == LAST[NC - 1, NKV - 2] + 2 and kind != "last":
                        for g in range(NKV - 1):
                            copy_v(b + 1, g)
                    for run, name in PLANS[kind][u]:
                        piece(kind, b, run, name)

            link(nc.gpsimd.memset(qT[:], 0.0))
            link(nc.gpsimd.memset(kT[:], 0.0))
            nc.gpsimd.memset(zero_rows[:], 0.0)
            link(nc.gpsimd.memset(v_pad[:], 0.0))
            nc.gpsimd.memset(v_pad[:, :, :, HD:HD + 1], 1.0).then_inc(zeroed, 1)
            for run, name in PRO:
                piece("before", -1, run, name)
            for g in range(NKV):
                copy_v(0, g)
            mask(0, 0)
            body("first", 0)
            with pool.Fori(1, B - 1) as b:
                body("steady", b)
            body("last", B - 1)
            for run, name in EPI:
                piece("after", B, run, name)
            for j in range(RING):
                pool.wait_ge(y_kept[j], 16 * (TILES // RING))
            pool.wait_ge(packed_ready, 1)
            base = state["n"]
            with pool.Fori(0, CHUNKS // 2) as m:
                state.update(n=base, b=m, per=2)
                for j in range(2):
                    pool.wait_ge(y_tok_read, m * 2 + j + 1)
                    hold()
                    link(nc.gpsimd.tensor_copy(index[:, j, :], packed[:, bass.ds((m * 2 + j) * TQ, TQ)]))
                    hold()
                    for q in range(TQ):
                        nc.gpsimd.indirect_dma_start(
                            y_tok[:, j, P * q:P * q + P], None, ys_rows,
                            bass.IndirectOffsetOnAxis(ap=index[:, j, q:q + 1], axis=0)).then_inc(gathered[j], 16)

        @block.scalar
        def _(act):
            for dst, src in LATE:
                act.dma_start(dst, src, allow_slow_non_contiguous=True).then_inc(late_loaded, 16)
            act.wait_ge(w_loaded, 16 * len(EARLY))
            act.sem_inc(scores_read, 2)
            nc.scalar.activation(lam[:], log_lam[:], ACT.Exp, scale=-1.0).then_inc(exp_neg, 1)
            act.wait_ge(w_scaled, 1)

            def piece(kind, at, run, name):
                L = fillings(kind, at, run)
                b, c = at + RUNS[run][0], RUNS[run][1]
                cc = b * NC + c
                if name in ("up0", "up1"):
                    k = int(name[-1])
                    filled_bank(act, L[name])
                    nc.scalar.activation(xs[:, c, k, :], M[L[name][0]][:], ACT.Copy,
                                         scale=one_minus_lam[:, k:k + 1]).then_inc(misc_read[L[name][0]], 1)
                elif name == "x1T":
                    filled_bank(act, L[name])
                    nc.scalar.activation(x1T[:], M[L[name][0]][:], ACT.Copy).then_inc(misc_read[L[name][0]], 1)
                elif name == "qT":
                    act.wait_ge(parts_ready, cc)
                    filled_bank(act, L[name])
                    nc.scalar.activation(q_scaled[:], M[L[name][0]][:], ACT.Copy, scale=qn_col[:]).then_inc(misc_read[L[name][0]], 1)
                elif name == "kT":
                    filled_bank(act, L[name])
                    nc.scalar.activation(k_scaled[:], M[L[name][0]][0:KW, :], ACT.Copy,
                                         scale=kn_col[:]).then_inc(misc_read[L[name][0]], 1)
                elif name == "gate":
                    act.wait_ge(gate_ready, cc + 1)
                    g = gate[:].rearrange("p q h d -> p (q h d)")
                    nc.scalar.activation(g, g, ACT.Tanh, scale=0.5).then_inc(gate_tanh, 1)
                elif name == "ogT":
                    filled_bank(act, L[name])
                    nc.scalar.activation(ogT[:], M[L[name][0]][:], ACT.Copy).then_inc(misc_read[L[name][0]], 1)
                elif name == "h2T":
                    filled_bank(act, L[name])
                    nc.scalar.activation(h2T[:], M[L[name][0]][:], ACT.Copy).then_inc(misc_read[L[name][0]], 1)

            def exps(b, u):
                w = UNITS[u]["w"]
                act.wait_ge(probs_used, b * NU + u + 1)
                for n in UNITS[u]["subs"]:
                    hs = SUBS[n][1]
                    act.wait_ge(scores_ready, b * NS + n + 1)
                    dst = probs[:, u % PROBS, hs[0]:hs[-1] + 1, 0:w]
                    two = S2[n % 2]
                    if w > CH // 2:
                        src = two[:, :, 0:w]
                    elif w == CH // 2:
                        src = two[:, :, :].rearrange("p a (h w) -> p (a h) w", w=w)
                    else:
                        src = two[:, 0, :].rearrange("p (h w) -> p h w", w=w)
                    nc.scalar.activation(dst, src, ACT.Exp, bias=shift[:], scale=float(HD) ** -0.5).then_inc(scores_read, 1)

            def body(kind, b):
                for u in range(NU):
                    if u + 1 < NU:
                        exps(b, u + 1)
                    elif kind != "last":
                        exps(b + 1, 0)
                    if u:
                        keep_outputs(b, u - 1)
                    elif kind != "first":
                        keep_outputs(b - 1, NU - 1)
                    for run, name in PLANS[kind][u]:
                        piece(kind, b, run, name)

            def keep_outputs(b, u):
                unit = UNITS[u]
                if unit["last"]:
                    act.wait_ge(probs_used, b * NU + u + 1 + PROBS)
                    nc.scalar.activation(oT[:, unit["g"], CH * unit["c"]:CH * unit["c"] + CH], O[unit["out"] % 2][:],
                                         ACT.Copy).then_inc(o_read, 1)

            for run, name in PRO:
                piece("before", -1, run, name)
            act.wait_ge(bias_split_ready, 1)
            for p in range(PARTS):
                act.dma_start(bias[p:p + 1, :, :], bias_split[:, p, :]).then_inc(bias_ready, 16)
            act.wait_ge(late_ready, 1)
            act.wait_ge(bias_ready, 16 * PARTS)
            exps(0, 0)
            body("first", 0)
            with act.Fori(1, B - 1) as b:
                body("steady", b)
            body("last", B - 1)
            keep_outputs(B - 1, NU - 1)
            for run, name in EPI:
                piece("after", B, run, name)

            def tile_step(k, j, it):
                i = j % 2
                act.wait_ge(up_ready, k + 1)
                need(act, hid_ready, k - 1)
                nc.scalar.activation(sig[:, i, :], PU[i][:, HID:], ACT.Sigmoid).then_inc(sig_ready, 1)
                turn_at(k + 1, (j + 1) % 2)
                keep(k - 2, (j - 2) % RING)

            def turn_at(k, i):
                need(act, up_ready, k - 1)
                act.wait_ge(x_turned, k + 1)
                nc.scalar.activation(xT[:, i, :], PX[i][:, 0:P], ACT.Copy).then_inc(xT_ready, 1)

            def keep(k, j):
                if isinstance(k, int) and k < 0:
                    return
                act.wait_ge(y_copied, k + 1)
                act.dma_start(ys_rows[bass.ds(k * P, P), :], y_sb[:, j, :]).then_inc(y_kept[j], 16)

            act.wait_ge(table_ready, 1)
            turn_at(0, 0)
            over_tiles(act, tile_step)
            for k in (TILES - 2, TILES - 1):
                keep(k, k % RING)

        @block.vector
        def _(dve):
            v = nc.vector
            state = dict(n=0, b=None, per=0)

            def link(ins):
                ins.then_inc(dve_step, 1)
                state["n"] += 1
                dve.wait_ge(dve_step, state["n"] if state["b"] is None else state["b"] * state["per"] + state["n"])

            def rsqrt(y, x, tmp):
                link(v.tensor_scalar(y.bitcast(I32), x.bitcast(I32), -0.5, RSQRT_MAGIC, ALU.mult, ALU.add))
                for _ in range(3):
                    link(v.scalar_tensor_tensor(tmp, y, -0.5, y, ALU.mult, ALU.mult))
                    link(v.tensor_tensor(tmp, tmp, x, ALU.mult))
                    link(v.scalar_tensor_tensor(y, tmp, 1.5, y, ALU.add, ALU.mult))

            dve.sem_inc(o_read, 2)
            dve.sem_inc(y_tok_read, 2)
            for j in range(2):
                dve.sem_inc(stored[j], 16)
            v.memset(ones_bf[:], 1.0)
            v.memset(seen[:], 0.0)
            v.memset(no_tokens[:], 0.0)
            dve.wait_ge(w_loaded, 16 * len(EARLY))
            dve.wait_ge(exp_neg, 1)
            link(v.tensor_scalar(lam[:], lam[:], 1.0, None, ALU.add))
            link(v.reciprocal(lam[:], lam[:]))
            link(v.tensor_scalar(one_minus_lam[:], lam[:], -1.0, 1.0, ALU.mult, ALU.add))
            link(v.tensor_scalar(d_col[:], d_col[:], 1.0, None, ALU.add))
            v.tensor_scalar(skip_diag[:], idm[:], d_col[:], None, ALU.mult)
            v.tensor_scalar(w_qkv[:], w_qkv[:], ln1_col[:], None, ALU.mult).then_inc(w_scaled, 1)

            def late_constants():
                dve.wait_ge(late_loaded, 16 * len(LATE))
                link(v.tensor_copy(bias_split[:, 0, :], bias_in[:]))
                link(v.tensor_tensor(bias_rest[:], bias_in[:], bias_split[:, 0, :], ALU.subtract))
                link(v.tensor_copy(bias_split[:, 1, :], bias_rest[:]))
                v.tensor_tensor(bias_split[:, 2, :], bias_rest[:], bias_split[:, 1, :], ALU.subtract).then_inc(bias_split_ready, 1)
                v.tensor_scalar(w_r[:], w_r[:], ln2_col[:], None, ALU.mult)
                link(v.tensor_tensor(bound[:], norm_rows[:, 0, :], norm_rows[:, 1, :], ALU.mult))
                link(v.scalar_tensor_tensor(bound[:], bound[:], -1.0, bound[:], ALU.mult, ALU.max))
                link(v.tensor_reduce(shift[:], bound[:], AX_X, ALU.max))
                link(v.tensor_scalar(shift[:], shift[:], -float(HD) ** 0.5, SHIFT_FROM, ALU.mult, ALU.add))
                v.tensor_scalar(shift[:], shift[:], 0.0, None, ALU.min).then_inc(late_ready, 1)
                w1f = w_1[:].rearrange("p e f -> p (e f)")
                v.tensor_scalar(w1f, w1f, ln2_col[:], None, ALU.mult)

            def stage_a(L, b, c, name):
                cc = b * NC + c
                if name in ("up0", "up1"):
                    k = int(name[-1])
                    if c:
                        dve.wait_ge(scan_done, cc * SH + (k + 1 - SH))
                    read_bank(dve, L[name])
                    v.tensor_tensor_scan(xs[:, c, k, :], lam[:, k:k + 1].to_broadcast([P, CH]), xs[:, c, k, :],
                                         0.0 if c == 0 else xs[:, c - 1, k, CH - 1:CH],
                                         ALU.mult, ALU.add).then_inc(scan_done, 1)
                elif name == "z":
                    z = M[L[name][0]]
                    filled_bank(dve, L[name])
                    for q in range(TQ):
                        ins = v.bn_stats(stats[:, q, :], z[:, P * q:P * q + P])
                    link(ins)
                    dve.sem_inc(dve_held, 1)
                    for q in range(TQ):
                        ins = v.bn_aggr(mv[:, q, :], stats[:, q, :])
                    link(ins)
                    v.tensor_scalar(ln_arg[:, 0:TQ], mv[:, :, 1], LN_EPS, None, ALU.add)
                    link(v.tensor_scalar(ln_arg[:, TQ:], mv[:, :, 1], 1.0 + RMS_EPS, LN_EPS * RMS_EPS, ALU.mult, ALU.add))
                    rsqrt(ln_rs[:], ln_arg[:], ln_tmp[:])
                    dve.wait_ge(x1_kept, cc)
                    for q in range(TQ):
                        ins = v.tensor_scalar(x1[:, q, :], z[:, P * q:P * q + P], mv[:, q, 0:1], ln_rs[:, q:q + 1],
                                              ALU.subtract, ALU.mult)
                    ins.then_inc(misc_read[L[name][0]], 1)
                    link(v.tensor_tensor(r1[:], ln_arg[:, 0:TQ], ln_rs[:, 0:TQ], ALU.mult))
                    link(v.tensor_tensor(r1[:], r1[:], ln_rs[:, TQ:], ALU.mult))
                    v.tensor_copy(resid[:, bass.ds(b * NT + TQ * c, TQ), :], x1[:]).then_inc(x1_kept, 1)
                elif name in ("qkv01", "qkv23"):
                    q0, w3, m = int(name[3]), QW + 2 * KW, M[L[name][0]]
                    dve.wait_ge(v_kept, cc)
                    filled_bank(dve, L[name])
                    for q in (q0, q0 + 1):
                        ins = v.scalar_tensor_tensor(qkv[:, q, :], m[:, w3 * (q - q0):w3 * (q - q0) + w3],
                                                     r1[:, q:q + 1], b_qkv[:], ALU.mult, ALU.add)
                    ins.then_inc(misc_read[L[name][0]], 1)
                    if name == "qkv23":
                        rope_and_norm(L, b, c)
                elif name == "kT":
                    span = slice(CH * c, CH * c + CH)
                    read_bank(dve, L["qT"])
                    read_bank(dve, L["kT"])
                    dve.wait_ge(spilled[c], b * SPILL)
                    both = ((q_scaled, q_parts), (k_scaled, k_parts))
                    for p in range(PARTS - 1):
                        for x, parts in both:
                            ins = v.tensor_copy(parts[:, p, span], x[:])
                        link(ins)
                        for x, parts in both:
                            dst = x[:] if p < PARTS - 2 else parts[:, PARTS - 1, span]
                            ins = v.tensor_tensor(dst, x[:], parts[:, p, span], ALU.subtract)
                        if p < PARTS - 2:
                            link(ins)
                    ins.then_inc(parts_ready, 1)

            def rope_and_norm(L, b, c):
                read_bank(dve, L["qkv01"])
                read_bank(dve, L["qkv23"])
                head = [P, TQ, NQ + NKV, HD]
                by_head = lambda ap: ap.rearrange("p q (h d) -> p q h d", d=HD)
                qk, ra, rb = by_head(qkv[:, :, 0:QW + KW]), by_head(rot_a[:]), by_head(rot_b[:])
                cos = cos_t[:, TQ * c:TQ * c + TQ, :].unsqueeze(2).to_broadcast(head)
                sin = sin_t[:, TQ * c:TQ * c + TQ, :].unsqueeze(2).to_broadcast(head)
                v.tensor_tensor(ra, qk, cos, ALU.mult)
                v.tensor_tensor(rb[:, :, :, 0:4], qk[:, :, :, 4:8], sin[:, :, :, 0:4], ALU.mult)
                link(v.tensor_tensor(rb[:, :, :, 4:8], qk[:, :, :, 0:4], sin[:, :, :, 4:8], ALU.mult))
                link(v.tensor_tensor(rot_a[:], rot_a[:], rot_b[:], ALU.add))
                link(v.tensor_tensor(rot_b[:], rot_a[:], rot_a[:], ALU.mult))
                link(v.tensor_reduce(hs_arg[:], rot_b[:].rearrange("p q (h d) -> p (q h) d", d=HD), AX_X, ALU.add))
                link(v.tensor_scalar(hs_arg[:], hs_arg[:], 1.0 / HD, RMS_EPS, ALU.mult, ALU.add))
                rsqrt(hs_rs[:], hs_arg[:], hs_tmp[:])
                rs = hs_rs[:].rearrange("p (q h) -> p q h", q=TQ).unsqueeze(3)
                v.tensor_tensor(by_head(qn[:]), ra[:, :, 0:NQ, :], rs[:, :, 0:NQ, :].to_broadcast([P, TQ, NQ, HD]), ALU.mult)
                v.tensor_tensor(by_head(kn[:]), ra[:, :, NQ:, :],
                                rs[:, :, NQ:, :].to_broadcast([P, TQ, NKV, HD]), ALU.mult).then_inc(qkn_ready, 1)

            def stage_c(L, b, c, name):
                cc = b * NC + c
                g = gate[:].rearrange("p q h d -> p q (h d)")
                if name in ("row0", "row1", "row2", "row3"):
                    q, bank = int(name[-1]), L[name][0]
                    m = M[bank][:, 0:NKV * RCOLS].rearrange("p (g x) -> p g x", x=RCOLS)
                    heads = m[:, :, 0:GH * RH].rearrange("p g (j y) -> p g j y", y=RH)
                    filled_bank(dve, L[name])
                    rd = r_den[:, q].rearrange("p (g j) -> p g j", j=GH)
                    link(v.reciprocal(rd, m[:, :, GH * RH:]))
                    rd = rd.unsqueeze(3).to_broadcast([P, NKV, GH, HD])
                    v.tensor_tensor(o_n[:, q].rearrange("p (g j) d -> p g j d", j=GH), heads[:, :, :, 0:HD], rd, ALU.mult)
                    v.tensor_tensor(gate[:, q].rearrange("p (g j) d -> p g j d", j=GH), heads[:, :, :, HD:], rd,
                                    ALU.mult).then_inc(misc_read[bank], 1)
                    if q == TQ - 1:
                        for name in ("row2", "row3"):
                            read_bank(dve, L[name])
                        v.tensor_tensor(g, g, bg_b[:].rearrange("p h d -> p (h d)").unsqueeze(1).to_broadcast([P, TQ, QW]),
                                        ALU.add).then_inc(gate_ready, 1)
                elif name == "gate":
                    dve.wait_ge(gate_tanh, cc + 1)
                    v.scalar_tensor_tensor(og[:], g, 1.0, o_n[:].rearrange("p q h d -> p q (h d)"),
                                           ALU.add, ALU.mult).then_inc(og_ready, 1)
                elif name == "proj":
                    tiles = bass.ds(b * NT + TQ * c, TQ)
                    dve.wait_ge(x1_kept, cc + 1)
                    dve.wait_ge(x2_kept, cc)
                    filled_bank(dve, L[name])
                    v.tensor_tensor(x2[:], M[L[name][0]][:].rearrange("p (q d) -> p q d", d=D), resid[:, tiles, :],
                                    ALU.add).then_inc(misc_read[L[name][0]], 1)
                    read_bank(dve, L[name])
                    link(v.tensor_tensor(x2[:], x2[:], bo_b[:].unsqueeze(1).to_broadcast([P, TQ, D]), ALU.add))
                    link(v.tensor_tensor(sq[:], x2[:], x2[:], ALU.mult))
                    link(v.tensor_reduce(r2_arg[:], sq[:], AX_X, ALU.add))
                    link(v.tensor_scalar(r2_arg[:], r2_arg[:], 1.0 / D, RMS_EPS, ALU.mult, ALU.add))
                    rsqrt(r2[:], r2_arg[:], r2_tmp[:])
                    dve.wait_ge(scattered, cc * (16 * TQ))
                    v.tensor_tensor(h2[:], x2[:], r2[:].unsqueeze(2).to_broadcast([P, TQ, D]),
                                    ALU.mult).then_inc(h2_ready, 1)
                elif name == "logits":
                    filled_bank(dve, L[name])
                    v.tensor_tensor(lg[:], M[L[name][0]][:, 0:TQ * E].rearrange("p (q e) -> p q e", e=E),
                                    br_b[:].unsqueeze(1).to_broadcast([P, TQ, E]), ALU.add).then_inc(misc_read[L[name][0]], 1)
                    read_bank(dve, L[name])
                    top = lg_max[:].unsqueeze(2).to_broadcast([P, TQ, E])
                    link(v.tensor_reduce(lg_max[:], lg[:], AX_X, ALU.max))
                    link(v.tensor_tensor(lg[:], lg[:], top, ALU.is_ge))
                    link(v.tensor_tensor(lg[:], lg[:], rank8[:].unsqueeze(1).to_broadcast([P, TQ, E]), ALU.mult))
                    link(v.tensor_reduce(lg_max[:], lg[:], AX_X, ALU.max))
                    link(v.tensor_tensor(onehot[:], lg[:], top, ALU.is_equal))
                    for q in range(TQ + 1):
                        ins = v.tensor_tensor(seen[:, q, :], seen[:, (q - 1) % (TQ + 1), :],
                                              onehot[:, q - 1, :] if q else no_tokens[:], ALU.add)
                        if q < TQ:
                            link(ins)
                    ins.then_inc(route_ready, 1)
                elif name == "rank":
                    filled_bank(dve, L[name])
                    v.tensor_tensor(slot_f[:], M[L[name][0]][:, 0:TQ * E].rearrange("p (q e) -> p q e", e=E),
                                    region_of[:].unsqueeze(1).to_broadcast([P, TQ, E]), ALU.add).then_inc(misc_read[L[name][0]], 1)
                    read_bank(dve, L[name])
                    link(v.tensor_tensor(slot_f[:], slot_f[:], onehot[:], ALU.mult))
                    link(v.tensor_reduce(slot_s[:], slot_f[:], AX_X, ALU.add))
                    dve.wait_ge(scattered, cc * (16 * TQ))
                    dve.wait_ge(slots_kept, cc)
                    dve.sem_inc(dve_held, 1)
                    v.tensor_copy(slot[:], slot_s[:]).then_inc(slot_ready, 1)

            def piece(kind, at, run, name):
                L = fillings(kind, at, run)
                b, c = at + RUNS[run][0], RUNS[run][1]
                if run[0] == "A":
                    stage_a(L, b, c, name)
                else:
                    stage_c(L, b, c, name)

            def body(kind, b):
                for u in range(NU):
                    for run, name in PLANS[kind][u]:
                        piece(kind, b, run, name)

            for run, name in PRO:
                piece("before", -1, run, name)
            late_constants()
            body("first", 0)
            base = state["n"]
            with dve.Fori(1, B - 1) as b:
                state.update(n=base - DVE_STEPS, b=b, per=DVE_STEPS)
                body("steady", b)
                assert state["n"] == base, state["n"] - base
            state.update(n=base + (B - 2) * DVE_STEPS, b=None)
            body("last", B - 1)
            for run, name in EPI:
                piece("after", B, run, name)
            dve.wait_ge(count_ready, 1)
            link(v.tensor_copy(count[:], PY[1][:, 0:E]))
            link(v.tensor_tensor(fill_row[:], count[0:1, :], region_of[0:1, :], ALU.add))
            over3 = [P, E, FULL]
            link(v.tensor_scalar(count[:], count[:], 1.0 / P, None, ALU.mult))
            link(v.tensor_tensor(over[:], count[:].unsqueeze(2).to_broadcast(over3),
                                 tile_steps[:].unsqueeze(1).to_broadcast(over3), ALU.is_gt))
            link(v.tensor_reduce(n_tiles[:], over[:], AX_X, ALU.add))
            link(v.tensor_tensor_scan(end_tile[:], ones_sq[:, 0:E], n_tiles[:], 0.0, ALU.mult, ALU.add))
            link(v.tensor_tensor(start_tile[:], end_tile[:], n_tiles[:], ALU.subtract))
            link(v.scalar_tensor_tensor(packed_off[:], start_tile[:], float(P), region_of[:], ALU.mult, ALU.subtract))
            v.tensor_copy(packed_step[:, 0:1], packed_off[:, 0:1])
            v.tensor_tensor(packed_step[:, 1:], packed_off[:, 1:], packed_off[:, 0:E - 1], ALU.subtract)
            link(v.tensor_scalar(region_a[:], packed_off[:], -1.0, -float(SPARE_BASE), ALU.mult, ALU.add))
            each = [1, ENTRIES, E]
            k3 = tile_no[:].unsqueeze(2).to_broadcast(each)
            link(v.tensor_tensor(mine[:], k3, start_tile[0:1, :].unsqueeze(1).to_broadcast(each), ALU.is_ge))
            link(v.tensor_tensor(mine_x[:], k3, end_tile[0:1, :].unsqueeze(1).to_broadcast(each), ALU.is_ge))
            link(v.tensor_tensor(mine[:], mine[:], mine_x[:], ALU.subtract))
            link(v.tensor_tensor(mine_x[:], mine[:], expert_no[:].unsqueeze(1).to_broadcast(each), ALU.mult))
            link(v.tensor_reduce(exp_f[:], mine_x[:], AX_X, ALU.add))
            v.tensor_copy(tile_expert[:], exp_f[:])
            link(v.tensor_tensor(mine_x[:], mine[:], region_a[0:1, :].unsqueeze(1).to_broadcast(each), ALU.mult))
            link(v.tensor_reduce(row_f[:], mine_x[:], AX_X, ALU.add))
            link(v.scalar_tensor_tensor(row_f[:], tile_no[:], float(P), row_f[:], ALU.mult, ALU.add))
            link(v.tensor_scalar(row_f[:], row_f[:], float(SPARE_BASE), None, ALU.add))
            v.tensor_copy(tile_row[:], row_f[:]).then_inc(table_ready, 1)
            dve.wait_ge(slots_kept, CHUNKS)
            dve.wait_ge(x2_kept, CHUNKS)
            all3 = [P, B * NT, E]
            link(v.tensor_tensor(slot_ge[:], slots[:].unsqueeze(2).to_broadcast(all3),
                                 region_of[:].unsqueeze(1).to_broadcast(all3), ALU.is_ge))
            link(v.tensor_tensor(slot_ge[:], slot_ge[:], packed_step[:].unsqueeze(1).to_broadcast(all3), ALU.mult))
            link(v.tensor_reduce(moved[:], slot_ge[:], AX_X, ALU.add))
            v.tensor_tensor(packed[:], slots[:], moved[:], ALU.add).then_inc(packed_ready, 1)

            def turned(k, i):
                dve.wait_ge(hid_turned, k + 1)
                need(dve, y_ready, k - 1)
                v.tensor_copy(hidT[:, i, :], PH[i][:, 0:HID]).then_inc(hidT_ready, 1)

            def gated(k, i):
                dve.wait_ge(sig_ready, k + 1)
                need(dve, hid_turned, k - 1)
                v.tensor_tensor(hid[:, i, :], PU[i][:, 0:HID], sig[:, i, :], ALU.mult).then_inc(hid_ready, 1)

            def result(k, j):
                dve.wait_ge(y_ready, k + 1)
                need(dve, y_kept[j], (k - j) // RING * 16 if isinstance(k, int) else (k - j) * (16 // RING))
                v.tensor_copy(y_sb[:, j, :], PY[j % 2][:, 0:D]).then_inc(y_copied, 1)

            def tile_step(k, j, it):
                first = isinstance(k, int)
                if not first or k >= 1:
                    turned(k - 1, (j - 1) % 2)
                gated(k, j % 2)
                if not first or k >= 2:
                    result(k - 2, (j - 2) % RING)

            over_tiles(dve, tile_step)
            turned(TILES - 1, (TILES - 1) % 2)
            result(TILES - 2, (TILES - 2) % RING)
            result(TILES - 1, (TILES - 1) % RING)

            base = state["n"]
            with dve.Fori(0, CHUNKS // 2) as m:
                state.update(n=base, b=m, per=DVE_STEPS_F)
                for j in range(2):
                    n = m * 2 + j
                    z = z2[:, j, :].rearrange("p (q d) -> p q d", d=D)
                    dve.wait_ge(gathered[j], m * (16 * TQ) + 16 * TQ)
                    v.tensor_tensor(z, y_tok[:, j, :].rearrange("p (q d) -> p q d", d=D),
                                    resid[:, bass.ds(n * TQ, TQ), :], ALU.add).then_inc(y_tok_read, 1)
                    dve.wait_ge(y_tok_read, n + 1 + 2)
                    for q in range(TQ):
                        ins = v.bn_stats(stats[:, q, :], z[:, q, :])
                    link(ins)
                    dve.sem_inc(dve_held, 1)
                    for q in range(TQ):
                        ins = v.bn_aggr(mv[:, q, :], stats[:, q, :])
                    link(ins)
                    link(v.tensor_scalar(r2_arg[:], mv[:, :, 1], LN_EPS, None, ALU.add))
                    rsqrt(r2[:], r2_arg[:], r2_tmp[:])
                    dve.wait_ge(stored[j], m * 16 + 16)
                    for q in range(TQ):
                        ins = v.tensor_scalar(y_out[:, j, P * q:P * q + P], z[:, q, :], mv[:, q, 0:1], r2[:, q:q + 1],
                                              ALU.subtract, ALU.mult)
                    ins.then_inc(y_final, 1)
                assert state["n"] - base == DVE_STEPS_F, state["n"] - base

        @block.tensor
        def _(pe):
            mm = nc.tensor.matmul
            pe.wait_ge(w_scaled, 1)
            pe.sem_inc(probs_used, PROBS)
            turn_tiles = lambda dst, src: [nc.tensor.transpose(dst[:, P * q:P * q + P], src[:, q, :], idm[:]) for q in range(TQ)][-1]

            def stage_a(L, b, c, name):
                cc = b * NC + c
                m, full = M[L[name][0]], misc_full[L[name][0]]
                if name in ("up0", "up1"):
                    k = int(name[-1])
                    pe.wait_ge(u_loaded[c], b * 16 + 16)
                    free_bank(pe, L[name])
                    mm(m[:], w_in[:, P * k:P * k + P], u_sb[:, c, :], start=True, stop=True).then_inc(full, 1)
                elif name == "z":
                    pe.wait_ge(scan_done, cc * SH + SH)
                    free_bank(pe, L[name])
                    for q in range(TQ):
                        tok = slice(P * q, P * q + P)
                        for k in range(SH):
                            mm(m[:, tok], xs[:, c, k, tok], w_out[:, k, :], start=k == 0, stop=False)
                        ins = mm(m[:, tok], u_sb[:, c, tok], skip_diag[:], start=False, stop=True)
                    ins.then_inc(full, 1)
                elif name == "x1T":
                    read_bank(pe, L["z"])
                    free_bank(pe, L[name])
                    turn_tiles(m, x1).then_inc(full, 1)
                elif name in ("qkv01", "qkv23"):
                    q0, w3 = int(name[3]), QW + 2 * KW
                    read_bank(pe, L["x1T"])
                    free_bank(pe, L[name])
                    for q in (q0, q0 + 1):
                        ins = mm(m[:, w3 * (q - q0):w3 * (q - q0) + w3], x1T[:, P * q:P * q + P], w_qkv[:], start=True, stop=True)
                    ins.then_inc(full, 1)
                elif name == "qT":
                    pe.wait_ge(qkn_ready, cc + 1)
                    free_bank(pe, L[name])
                    turn_tiles(m, qn).then_inc(full, 1)
                elif name == "kT":
                    free_bank(pe, L[name])
                    turn_tiles(m[0:KW, :], kn).then_inc(full, 1)

            def stage_c(L, b, c, name):
                cc = b * NC + c
                m, full = M[L[name][0]], misc_full[L[name][0]]
                if name in ("row0", "row1", "row2", "row3"):
                    q = int(name[-1])
                    pe.wait_ge(o_read, b * NO + NKV * (c + 1) + 2)
                    free_bank(pe, L[name])
                    for g in range(NKV):
                        t = CH * c + P * q
                        ins = mm(m[:, RCOLS * g:RCOLS * g + RCOLS], oT[:, g, t:t + P], mix[:], start=True, stop=True)
                    ins.then_inc(full, 1)
                elif name == "ogT":
                    pe.wait_ge(og_ready, cc + 1)
                    free_bank(pe, L[name])
                    turn_tiles(m, og).then_inc(full, 1)
                elif name == "proj":
                    read_bank(pe, L["ogT"])
                    free_bank(pe, L[name])
                    for q in range(TQ):
                        ins = mm(m[:, P * q:P * q + P], ogT[:, P * q:P * q + P], w_o[:], start=True, stop=True)
                    ins.then_inc(full, 1)
                elif name == "h2T":
                    pe.wait_ge(h2_ready, cc + 1)
                    free_bank(pe, L[name])
                    turn_tiles(m, h2).then_inc(full, 1)
                elif name == "logits":
                    read_bank(pe, L["h2T"])
                    free_bank(pe, L[name])
                    for q in range(TQ):
                        ins = mm(m[:, E * q:E * q + E], h2T[:, P * q:P * q + P], w_r[:], start=True, stop=True)
                    ins.then_inc(full, 1)
                elif name == "rank":
                    pe.wait_ge(route_ready, cc + 1)
                    free_bank(pe, L[name])
                    rank = m[:, 0:TQ * E]
                    mm(rank, before[:], onehot[:].rearrange("p q e -> p (q e)"), start=True, stop=False)
                    mm(rank, ones_sq[:], seen[:, 0:TQ, :].rearrange("p q e -> p (q e)"), start=False, stop=True).then_inc(full, 1)

            def piece(kind, at, run, name):
                if name in BANKLESS:
                    return
                L = fillings(kind, at, run)
                b, c = at + RUNS[run][0], RUNS[run][1]
                if run[0] == "A":
                    stage_a(L, b, c, name)
                else:
                    stage_c(L, b, c, name)

            def score(b, n):
                u, hs = SUBS[n]
                unit = UNITS[u]
                w, g, c = unit["w"], unit["g"], unit["c"]
                key = kT[:, g, P * unit["i"]:P * unit["i"] + P]
                if unit["first"]:
                    pe.wait_ge(stacked[c][g], b * STACK + STACK)
                pe.wait_ge(scores_read, b * NS + n + 1)
                per_bank = max(1, CH // w)
                for a in range(0, len(hs), per_bank):
                    k = min(per_bank, len(hs) - a)
                    h0 = GH * g + hs[a]
                    dst = S2[n % 2][:, a // per_bank, 0:k * w]
                    ins = mm(dst, key, qT[:, c, h0:h0 + k, CH - w:], start=True, stop=True)
                ins.then_inc(scores_ready, 1)

            def weigh(b, u):
                unit = UNITS[u]
                w, g, c = unit["w"], unit["g"], unit["c"]
                if unit["first"]:
                    pe.wait_ge(o_read, b * NO + unit["out"] + 1)
                    if c == 0:
                        pe.wait_ge(v_copied, b * NKV + g + 1)
                if unit["diag"]:
                    pe.wait_ge(probs_masked, b * NM + unit["masks_before"] + 1)
                else:
                    pe.wait_ge(scores_read, b * NS + unit["subs"][-1] + 1 + 2)
                for j in range(GH):
                    ins = mm(O[unit["out"] % 2][32 * j:32 * j + 32, CH - w:CH], v_pad[:, unit["i"], g, :], probs[:, u % PROBS, j, 0:w],
                             start=unit["first"], stop=unit["last"], tile_position=(0, 32 * j))
                ins.then_inc(probs_used, 1)

            def body(kind, b):
                for u in range(NU):
                    nb, nu = (b, u + 1) if u + 1 < NU else (b + 1, 0)
                    ahead = UNITS[nu]["subs"] if u + 1 < NU or kind != "last" else []
                    for n in ahead[:1]:
                        score(nb, n)
                    if u:
                        weigh(b, u - 1)
                    elif kind != "first":
                        weigh(b - 1, NU - 1)
                    for run, name in PLANS[kind][u]:
                        piece(kind, b, run, name)
                    for n in ahead[1:]:
                        score(nb, n)

            for run, name in PRO:
                piece("before", -1, run, name)
            pe.wait_ge(late_ready, 1)
            for n in UNITS[0]["subs"]:
                score(0, n)
            body("first", 0)
            with pe.Fori(1, B - 1) as b:
                body("steady", b)
            body("last", B - 1)
            weigh(B - 1, NU - 1)
            for run, name in EPI:
                piece("after", B, run, name)
            mm(PY[1][:, 0:E], ones_sq[:], seen[:, TQ, :], start=True, stop=True).then_inc(count_ready, 1)

            def turn(k, j, it):
                pe.wait_ge(x_loaded[j], it * 16 + 16)
                need(pe, xT_ready, k - 1)
                nc.tensor.transpose(PX[j % 2][:, 0:P], x_in[:, j, :], idm[:]).then_inc(x_turned, 1)

            def up(k, j):
                e = pe.value_load(tile_expert[0:1, bass.ds(k, 1)], min_val=0, max_val=E - 1)
                pe.wait_ge(xT_ready, k + 1)
                need(pe, hid_ready, k - 1)
                mm(PU[j % 2], xT[:, j % 2, :], w_1[:, bass.ds(e, 1), :].squeeze(1), start=True, stop=False)
                mm(PU[j % 2], ones_bf[:], bias[:, bass.ds(e, 1), 0:2 * HID].squeeze(1), start=False, stop=True).then_inc(up_ready, 1)

            def turn_hidden(k, j):
                pe.wait_ge(hid_ready, k + 1)
                need(pe, hidT_ready, k - 1)
                for f in range(2):
                    ins = nc.tensor.transpose(PH[j % 2][:, P * f:P * f + P], hid[:, j % 2, P * f:P * f + P], idm[:])
                ins.then_inc(hid_turned, 1)

            def down(k, j):
                e = pe.value_load(tile_expert[0:1, bass.ds(k, 1)], min_val=0, max_val=E - 1)
                pe.wait_ge(hidT_ready, k + 1)
                need(pe, y_copied, k - 1)
                y = PY[j % 2][:, 0:D]
                for f in range(2):
                    mm(y, hidT[:, j % 2, P * f:P * f + P], w_2[:, bass.ds(e, 1), f, :].squeeze(1), start=f == 0, stop=False)
                mm(y, ones_bf[:], bias[:, bass.ds(e, 1), 2 * HID:].squeeze(1), start=False, stop=True).then_inc(y_ready, 1)

            def tile_step(k, j, it):
                first = isinstance(k, int)
                up(k, j)
                if not first or k >= 1:
                    turn_hidden(k - 1, (j - 1) % RING)
                if not first or k >= 2:
                    down(k - 2, (j - 2) % RING)
                turn(k + 1, (j + 1) % RING, it + (j + 1) // RING)

            pe.wait_ge(bias_ready, 16 * PARTS)
            pe.wait_ge(table_ready, 1)
            turn(0, 0, 0)
            over_tiles(pe, tile_step)
            turn_hidden(TILES - 1, (TILES - 1) % RING)
            down(TILES - 2, (TILES - 2) % RING)
            down(TILES - 1, (TILES - 1) % RING)


DVE_STEPS = 124
DVE_STEPS_F = 26

_ORDER = ["uT", "WinT", "log_lambda", "WoutT", "Dvec", "ln1_w", "ln2_w", "Wq", "bq", "Wk", "bk", "Wv", "bv", "qn_w",
          "kn_w", "gate_mix", "bg", "Wo", "bo", "Wr", "br", "W1", "b1", "W2", "b2", "ident", "cos8", "sin8", "first_of",
          "all_ones", "earlier", "regions", "tile_nos", "expert_nos"]


def shape_constants():
    inv_freq = (np.float32(1.0) / np.float32(10000.0) ** (np.arange(0, HD, 2, dtype=np.float32) / np.float32(HD))).astype(np.float32)
    ang = np.arange(T, dtype=np.float32)[:, None] * inv_freq[None, :]
    c, s = np.cos(ang).astype(np.float32), np.sin(ang).astype(np.float32)
    tiled = lambda a: np.ascontiguousarray(a.reshape(NT, P, HD).transpose(1, 0, 2))
    return {"ident": np.eye(P, dtype=np.float32), "cos8": tiled(np.concatenate([c, c], 1)),
            "sin8": tiled(np.concatenate([-s, s], 1)), "first_of": np.arange(E, 0, -1).astype(np.float32),
            "all_ones": np.ones((P, P), np.float32), "earlier": np.triu(np.ones((P, P), np.float32), 1),
            "regions": (np.arange(E) * REGION).astype(np.float32), "tile_nos": np.arange(ENTRIES).astype(np.float32),
            "expert_nos": np.arange(E).astype(np.float32)}


def kernel(**inputs):
    import concourse.bacc as bacc
    from concourse.bass_utils import run_bass_kernel_spmd

    a = {k.replace("L0_attn_", "").replace("L0_ffn_", ""): np.asarray(x) for k, x in inputs.items()}
    gate_mix = np.zeros((P, RCOLS), np.float32)
    for j in range(GH):
        gate_mix[32 * j:32 * j + HD, RH * j:RH * j + HD] = np.diag(np.full(HD, 0.5, np.float32))
        gate_mix[32 * j:32 * j + HD, RH * j + HD:RH * j + RH] = a["Wg"]
        gate_mix[32 * j + HD, GH * RH + j] = 1.0
    arrays = {"uT": a["u"].transpose(0, 2, 1), "WinT": a["W_in"].T, "WoutT": a["W_out"].T, "Dvec": a["D"],
              "gate_mix": gate_mix, **shape_constants()}
    for name in _ORDER:
        if name not in arrays:
            arrays[name] = a[name]
    nc = bacc.Bacc("TRN2", target_bir_lowering=False, num_devices=1)
    feed, args = {}, []
    for name in _ORDER:
        x = np.ascontiguousarray(arrays[name])
        feed[f"in_{name}"] = x
        args.append(nc.dram_tensor(f"in_{name}", x.shape, mybir.dt.from_np(x.dtype), kind="ExternalInput").ap())
    out = nc.dram_tensor("out", (CHUNKS, P, TQ, D), F32, kind="ExternalOutput").ap()
    block_kernel(nc, *args, out)
    r = run_bass_kernel_spmd(nc, [feed], core_ids=[0])
    got = np.asarray(r.results[0]["out"])
    return got.transpose(0, 2, 1, 3).reshape(B, T, D)
```

```python
from contextlib import ExitStack

import numpy as np

import concourse.bass as bass
from concourse import mybir

F32 = mybir.dt.float32
BF16 = mybir.dt.bfloat16
I32 = mybir.dt.int32
ALU = mybir.AluOpType
ACT = mybir.ActivationFunctionType
AX_X = mybir.AxisListType.X

P = 128
B, T, D = 4, 1024, 128
STATE = 256
SH = STATE // P
NQ, NKV, HD = 16, 4, 8
GH = NQ // NKV
QW, KW = NQ * HD, NKV * HD
HID, E = 256, 8
LN_EPS, RMS_EPS = 1e-5, 1e-6
CH = 512
NC = T // CH
TQ = CH // P
NT = T // P
CHUNKS = B * NC
RSQRT_MAGIC = float(0x5F3759DF)
SHIFT_FROM = 60.0

PARTS = 3
TERMS = PARTS * PARTS

RH = 2 * HD
RCOLS = GH * RH + GH

TOKENS = B * T
REGION = TOKENS + P
SPARE = E * REGION
FULL = TOKENS // P
TILES = TOKENS // P + E
RING = 8
GROUP = 4
PAIR = 2
ROW = 2 * D + 4
BIAS = 2 * HID + D
assert TILES % RING == 0
SPARE_BASE = SPARE - FULL * P
ENTRIES = TILES + 2
ROWS = SPARE_BASE + ENTRIES * P


def attention_units():
    units, subs = [], []
    for c in range(NC):
        for g in range(NKV):
            last = TQ * (c + 1) - 1
            for i in range(last + 1):
                width = CH - P * max(0, i - TQ * c)
                unit = dict(g=g, c=c, i=i, w=width, diag=i >= TQ * c, first=i == 0, last=i == last, subs=[],
                            out=c * NKV + g)
                heads = [(0, 1), (2, 3)] if width > CH // 2 else [(0, 1, 2, 3)]
                for hs in heads:
                    unit["subs"].append(len(subs))
                    subs.append((len(units), hs))
                units.append(unit)
    n = 0
    for u in units:
        u["masks_before"] = n
        n += u["diag"]
    return units, subs


UNITS, SUBS = attention_units()
NU, NS, NM = len(UNITS), len(SUBS), sum(u["diag"] for u in UNITS)
NO = NC * NKV
LAST = {(u["c"], u["g"]): n for n, u in enumerate(UNITS) if u["last"]}
PROBS = 3
assert NU % PROBS == 0 and NS % 2 == 0 and NO % 2 == 0

RUNS = {"A0": (1, 0), "A1": (1, 1), "C1": (-1, 1), "C0": (0, 0), "P1": (0, 1)}
BANKLESS = ("gate", "scatter0", "scatter1", "scatter2", "scatter3")
AT_A = dict(up0=0, up1=1, z=11, x1T=34, qkv01=38, qkv23=39, qT=66, kT=68)
AT_C = dict(row0=5, row1=7, row2=9, row3=11, gate=35, ogT=37, proj=45, h2T=83, logits=87, rank=96,
            scatter0=98, scatter1=98.5, scatter2=99, scatter3=99.5)
AT_P1 = dict(qkv01=0, qkv23=1, qT=20, kT=21)
AT_A0 = dict(up0=25, up1=26, z=34, x1T=50, qkv01=54, qkv23=55, qT=78, kT=80)


def unit_work(unit):
    return len(unit["subs"]) * 0.19 + GH * unit["w"] * 0.833e-3


def plan(first_half, second_half):
    total, now = sum(unit_work(u) for u in UNITS), 0.0
    start = []
    for unit in UNITS:
        start.append(now / total * 200)
        now += unit_work(unit)
    pieces = []
    for half, runs in enumerate((first_half, second_half)):
        for run, at in runs:
            pieces += [(100 * half + t, run, name) for name, t in at.items()]
    pieces.sort(key=lambda x: x[0])
    steps, u = [[] for _ in UNITS], 0
    for t, run, name in pieces:
        while u + 1 < NU and (start[u] < t or sum(n not in BANKLESS for _, n in steps[u]) >= 2
                              or (run[0] == "C" and any(r == run for r, _ in steps[u]) and u < NU - 1)):
            u += 1
        steps[u].append((run, name))
    return steps


FIRST = dict(w_in=STATE, log_lam=SH, d_col=1, ln1_col=1, qn_col=1, kn_col=1, idm=P)
SECOND = dict(w_out=SH * D, w_qkv=QW + 2 * KW, b_qkv=QW + 2 * KW, cos_t=NT * HD, sin_t=NT * HD)
LATE = dict(mix=RCOLS, w_o=D, bo_b=D, w_r=E, br_b=E, rank8=E, ones_sq=P, before=P, region_of=E, tile_steps=FULL,
            bg_b=NQ * HD, norm_rows=2 * HD, ln2_col=1, token_no=B * NT + TILES, tile_no=ENTRIES, expert_no=E)


A0, A1, C0, C1 = ("A0", AT_A), ("A1", AT_A), ("C0", AT_C), ("C1", AT_C)
PLANS = {"first": plan((("P1", AT_P1), ("A0", AT_A0)), (A1, C0)), "steady": plan((A0, C1), (A1, C0)), "last": plan((C1,), (C0,))}
UPS = ("up0", "up1")
PRO = [("A0", n) for n in UPS] + [("A1", n) for n in UPS] + [("A0", n) for n in ("z", "x1T", "qkv01", "qkv23", "qT", "kT")] \
    + [("A1", "z"), ("A1", "x1T")]
EPI = [("C1", n) for n in AT_C]


def number(pieces):
    return {p: j for j, p in enumerate([p for p in pieces if p[1] not in BANKLESS])}


FILLS = {"before": number(PRO), "after": number(EPI), **{k: number(sum(v, [])) for k, v in PLANS.items()}}
N_FIRST = len(FILLS["before"])
N_STEADY = len(FILLS["steady"])
N_OFF = N_FIRST + len(FILLS["first"]) - N_STEADY
assert N_STEADY % 2 == 0


def fillings(kind, b, run):
    where = fillings("before", -1, "A1") if run == "P1" else {}
    for (r, name), j in FILLS[kind].items():
        if r != run:
            continue
        if kind in ("before", "first"):
            n = j + (N_FIRST if kind == "first" else 0)
            where[name] = n % 2, n // 2
        else:
            j += N_OFF
            if kind == "after":
                j -= N_STEADY - len(FILLS["last"])
            where[name] = j % 2, b * (N_STEADY // 2) + j // 2
    return where


def block_kernel(nc, uT, first_in, second_in, late_in, W1, b1, W2, b2, out):
    with ExitStack() as ctx:
        def sb(name, shape, dt=F32):
            return ctx.enter_context(nc.sbuf_tensor(name, shape, dt))

        def sem(name):
            return ctx.enter_context(nc.semaphore(name))

        def fields(name, columns):
            whole = sb(name, [P, sum(columns.values())])
            views, at = {}, 0
            for field, n in columns.items():
                views[field] = whole[:, at:at + n]
                at += n
            return whole, views

        first, f = fields("first", FIRST)
        second, s = fields("second", SECOND)
        late, l = fields("late", LATE)
        w_in, log_lam, d_col, ln1_col, qn_col, idm = (f[n] for n in ("w_in", "log_lam", "d_col", "ln1_col", "qn_col", "idm"))
        kn_col = f["kn_col"][0:KW]
        w_out, w_qkv, b_qkv = s["w_out"].rearrange("p (k d) -> p k d", d=D), s["w_qkv"], s["b_qkv"]
        cos_t, sin_t = (s[n].rearrange("p (t d) -> p t d", d=HD) for n in ("cos_t", "sin_t"))
        mix, w_o, bo_b, w_r, br_b, rank8 = (l[n] for n in ("mix", "w_o", "bo_b", "w_r", "br_b", "rank8"))
        ones_sq = l["ones_sq"]
        before = l["before"]
        region_of = l["region_of"]
        tile_steps, ln2_col, token_no = l["tile_steps"], l["ln2_col"], l["token_no"]
        bg_b = l["bg_b"]
        norm_rows = l["norm_rows"].rearrange("p (n d) -> p n d", d=HD)
        tile_no, expert_no = l["tile_no"][0:1], l["expert_no"][0:1]
        lam = sb("lam", [P, SH])
        one_minus_lam = sb("one_minus_lam", [P, SH])
        skip_diag = sb("skip_diag", [P, P])
        bound = sb("bound", [P, HD])
        shift = sb("shift", [P, 1])
        w_1 = sb("w_1", [P, E, 2 * HID])
        bias = sb("bias", [PARTS, E, BIAS], BF16)
        ones_bf = sb("ones_bf", [PARTS, P], BF16)
        zero_rows = sb("zero_rows", [P, ROW])
        w_2 = sb("w_2", [P, E, 2, D])

        u_sb = sb("u_sb", [P, NC, CH])
        xs = sb("xs", [P, NC, SH, CH])
        stats = sb("stats", [P, TQ, 6])
        mv = sb("mv", [P, TQ, 2])
        ln_arg = sb("ln_arg", [P, 2 * TQ])
        ln_rs = sb("ln_rs", [P, 2 * TQ])
        ln_tmp = sb("ln_tmp", [P, 2 * TQ])
        r1 = sb("r1", [P, TQ])
        x1 = sb("x1", [P, TQ, D])
        x1T = sb("x1T", [P, CH])
        qkv = sb("qkv", [P, TQ, QW + 2 * KW])
        rot_a = sb("rot_a", [P, TQ, QW + KW])
        rot_b = sb("rot_b", [P, TQ, QW + KW])
        hs_arg = sb("hs_arg", [P, TQ * (NQ + NKV)])
        hs_rs = sb("hs_rs", [P, TQ * (NQ + NKV)])
        hs_tmp = sb("hs_tmp", [P, TQ * (NQ + NKV)])
        qn = sb("qn", [P, TQ, QW])
        kn = sb("kn", [P, TQ, KW])
        q_scaled = sb("q_scaled", [P, CH])
        k_scaled = sb("k_scaled", [KW, CH])
        v_next = sb("v_next", [P, NT, KW])
        q_parts = sb("q_parts", [P, PARTS, T], BF16)
        k_parts = sb("k_parts", [KW, PARTS, T], BF16)
        resid = sb("resid", [P, B * NT, D])

        q_spill = nc.dram_tensor("q_spill", (NC, PARTS, HD, NQ, CH), BF16, kind="Internal").ap()
        k_spill = nc.dram_tensor("k_spill", (NC, NKV, PARTS, HD, CH), BF16, kind="Internal").ap()

        qT = sb("qT", [P, NC, NQ, CH], BF16)
        kT = sb("kT", [P, NKV, T], BF16)
        v_pad = sb("v_pad", [P, NT, NKV, 32])
        probs = sb("probs", [P, PROBS, GH, CH])
        oT = sb("oT", [P, NKV, T])
        early = probs[0:E].rearrange("e n j t -> e (n j t)")
        bias_in, bias_rest = early[:, 0:BIAS], early[:, BIAS:2 * BIAS]
        bias_split = early[:, 2 * BIAS:2 * BIAS + PARTS * BIAS // 2].bitcast(BF16).rearrange("e (p x) -> e p x", p=PARTS)

        r_den = sb("r_den", [P, TQ, NQ])
        o_n = sb("o_n", [P, TQ, NQ, HD])
        gate = sb("gate", [P, TQ, NQ, HD])
        og = sb("og", [P, TQ, QW])
        ogT = sb("ogT", [P, CH])
        x2 = sb("x2", [P, TQ, D])
        sq = og
        r2_arg = sb("r2_arg", [P, TQ])
        r2 = sb("r2", [P, TQ])
        r2_tmp = sb("r2_tmp", [P, TQ])
        routed = sb("routed", [P, TQ, ROW])
        h2, last_resid, number = routed[:, :, 0:D], routed[:, :, D:2 * D], routed[:, :, 2 * D:2 * D + 1]
        h2T = sb("h2T", [P, CH])
        lg = sb("lg", [P, TQ, E])
        lg_max = sb("lg_max", [P, TQ])
        onehot = sb("onehot", [P, TQ, E])
        no_tokens = sb("no_tokens", [P, E])
        seen = sb("seen", [P, TQ + 1, E])
        slot_f = sb("slot_f", [P, TQ, E])
        slot_s = sb("slot_s", [P, TQ])
        slot = sb("slot", [P, TQ], I32)
        xs_rows = nc.dram_tensor("xs_rows", (ROWS, ROW), F32, kind="Internal").ap()

        count = sb("count", [P, E])
        n_tiles = sb("n_tiles", [P, E])
        end_tile = sb("end_tile", [P, E])
        start_tile = sb("start_tile", [P, E])
        region_a = sb("region_a", [1, E])
        row_f = sb("row_f", [1, ENTRIES])
        exp_f = sb("exp_f", [1, ENTRIES])
        tile_row = sb("tile_row", [1, ENTRIES], I32)
        tile_expert = sb("tile_expert", [1, ENTRIES], I32)
        fill_row = sb("fill_row", [1, E], I32)
        carve = oT[:].rearrange("p g t -> p (g t)")
        over = carve[:, 3072:3328].rearrange("p (e n) -> p e n", e=E)
        mine = carve[0:1, 3328:3328 + ENTRIES * E].rearrange("p (k e) -> p k e", e=E)
        mine_x = carve[0:1, 3696:3696 + ENTRIES * E].rearrange("p (k e) -> p k e", e=E)
        xT = carve[:, 0:256].rearrange("p (n d) -> p n d", d=D)
        sig = carve[:, 256:768].rearrange("p (n d) -> p n d", d=HID)
        hid = carve[:, 768:1280].rearrange("p (n d) -> p n d", d=HID)
        hidT = carve[:, 1280:1792].rearrange("p (n d) -> p n d", d=HID)
        z_stats = carve[:, 1792:1792 + 6 * RING].rearrange("p (n x) -> p n x", x=6)
        z_mv = carve[:, 1856:1856 + 2 * RING].rearrange("p (n x) -> p n x", x=2)
        z_arg, z_rs, z_tmp = [carve[:, 1920 + RING * i:1920 + RING * i + RING] for i in range(3)]
        x_in = probs[:, 0:2].rearrange("p n j t -> p (n j t)")[:, 0:RING * ROW].rearrange("p (n x) -> p n x", x=ROW)
        x_number = x_in[:, :, 2 * D:2 * D + 1]
        late_probs = probs[:, 2].rearrange("p j t -> p (j t)")
        z = late_probs[:, 0:RING * D].rearrange("p (n d) -> p n d", d=D)
        z_out = carve[:, 1984:1984 + RING * D].rearrange("p (n d) -> p n d", d=D)
        number_kept = sb("number_kept", [P, RING])
        number_spare = sb("number_spare", [P, RING])
        number_out = sb("number_out", [P, RING], I32)

        S2 = [ctx.enter_context(nc.psum_tensor(f"scores{i}", [P, 2, CH], F32)) for i in range(2)]
        O = [ctx.enter_context(nc.psum_tensor(f"outputs{i}", [P, CH], F32)) for i in range(2)]
        M = [ctx.enter_context(nc.psum_tensor(f"misc{i}", [P, CH], F32)) for i in range(2)]
        PX, PU, PH, PY = M, [S2[0][:, i, :] for i in range(2)], [S2[1][:, i, :] for i in range(2)], O

        first_loaded = sem("first_loaded")
        second_loaded = sem("second_loaded")
        lam_ready = sem("lam_ready")
        u_loaded = [sem(f"u_loaded{c}") for c in range(NC)]
        late_loaded = sem("late_loaded")
        w_scaled = sem("w_scaled")
        late_ready = sem("late_ready")
        zeroed = sem("zeroed")
        misc_full = [sem(f"misc_full{i}") for i in range(2)]
        misc_read = [sem(f"misc_read{i}") for i in range(2)]
        scan_done = sem("scan_done")
        dve_step = sem("dve_step")
        pool_step = sem("pool_step")
        pool_held = sem("pool_held")
        dve_held = sem("dve_held")
        sp_held = sem("sp_held")
        qkn_ready = sem("qkn_ready")
        x1_kept = sem("x1_kept")
        parts_ready = sem("parts_ready")
        x2_kept = sem("x2_kept")
        v_kept = sem("v_kept")
        v_copied = sem("v_copied")
        first_v1_copied = sem("first_v1_copied")
        spilled = [sem(f"spilled{c}") for c in range(NC)]
        stacked = [[sem(f"stacked{c}_{g}") for g in range(NKV)] for c in range(NC)]
        scores_ready = sem("scores_ready")
        scores_read = sem("scores_read")
        probs_masked = sem("probs_masked")
        probs_used = sem("probs_used")
        o_read = sem("o_read")
        gate_ready = sem("gate_ready")
        gate_tanh = sem("gate_tanh")
        og_ready = sem("og_ready")
        h2_ready = sem("h2_ready")
        exp_neg = sem("exp_neg")
        bias_split_ready = sem("bias_split_ready")
        bias_ready = sem("bias_ready")
        route_ready = sem("route_ready")
        slot_ready = sem("slot_ready")
        scattered = sem("scattered")
        count_ready = sem("count_ready")
        rows_ready = sem("rows_ready")
        table_ready = sem("table_ready")
        fill_ready = sem("fill_ready")
        filled = sem("filled")
        x_loaded = [sem(f"x_loaded{i}") for i in range(RING)]
        x_turned = sem("x_turned")
        xT_ready = sem("xT_ready")
        up_ready = sem("up_ready")
        sig_ready = sem("sig_ready")
        hid_ready = sem("hid_ready")
        hid_turned = sem("hid_turned")
        hidT_ready = sem("hidT_ready")
        y_ready = sem("y_ready")
        z_ready = sem("z_ready")
        z_counted = sem("z_counted")
        out_ready = sem("out_ready")
        out_stored = [sem(f"out_stored{i}") for i in range(RING)]

        def filled_bank(eng, place):
            eng.wait_ge(misc_full[place[0]], place[1] + 1)

        def read_bank(eng, place):
            eng.wait_ge(misc_read[place[0]], place[1] + 1)

        def free_bank(eng, place):
            eng.wait_ge(misc_read[place[0]], place[1])

        def need(eng, sem, n):
            if not (isinstance(n, int) and n <= 0):
                eng.wait_ge(sem, n)

        def fill(eng, experts):
            eng.wait_ge(fill_ready, 1)
            for e in experts:
                r = eng.value_load(fill_row[0:1, e:e + 1], min_val=0, max_val=ROWS - P)
                eng.dma_start(xs_rows[bass.ds(r, P), :], zero_rows[:]).then_inc(filled, 16)

        def over_tiles(eng, step):
            for j in range(RING):
                step(j, j, 0)
            with eng.Fori(1, TILES // RING) as it:
                for j in range(RING):
                    step(it * RING + j, j, it)

        LATE_DMAS = 5

        block = ctx.enter_context(nc.Block())

        SPILL = 16 * 2 * PARTS
        STACK = 16 * (PARTS + 1)

        @block.sync
        def _(sp):
            def load_u(b, c, later=0):
                sp.dma_start(u_sb[:, c, :], uT[later:][b, :, CH * c:CH * c + CH]).then_inc(u_loaded[c], 16)

            def spill(b, c, later=0):
                span = slice(CH * c, CH * c + CH)
                for g in range(NKV):
                    sp.wait_ge(stacked[c][g], b * STACK + later * STACK)
                sp.wait_ge(parts_ready, b * NC + (later * NC + c + 1))
                for p in range(PARTS):
                    sp.dma_start(q_spill[c, p].rearrange("d h t -> h d t"), q_parts[:, p, span]).then_inc(spilled[c], 16)
                for p in range(PARTS):
                    sp.dma_start(k_spill[c, :, p], k_parts[:, p, span]).then_inc(spilled[c], 16)

            def stack(b, c, g, later=0):
                span = slice(CH * c, CH * c + CH)
                if later:
                    sp.wait_ge(scores_ready, b * NS + (UNITS[LAST[NC - 1, g]]["subs"][-1] + 1))
                sp.wait_ge(spilled[c], b * SPILL + (later * SPILL + SPILL))
                for p in range(PARTS):
                    src = q_spill[c, p:p + 1, :, GH * g:GH * g + GH, :].rearrange("a d h t -> a d (h t)")
                    sp.dma_start(qT[HD * PARTS * p:HD * PARTS * (p + 1), c, GH * g:GH * g + GH, :],
                                 src.to_broadcast([PARTS, HD, GH * CH])).then_inc(stacked[c][g], 16)
                src = k_spill[c, g:g + 1].rearrange("a p d t -> a (p d) t")
                sp.dma_start(kT[0:HD * TERMS, g, span], src.to_broadcast([PARTS, PARTS * HD, CH])).then_inc(stacked[c][g], 16)

            def body(b, prefetch):
                if prefetch:
                    sp.wait_ge(x1_kept, b * NC + 3)
                    sp.sem_inc(sp_held, 1)
                    load_u(b, 0, 2)
                spill(b, 0, 1)
                stack(b, 0, 0, 1)
                if prefetch:
                    sp.wait_ge(x1_kept, b * NC + 4)
                    sp.sem_inc(sp_held, 1)
                    load_u(b, 1, 2)
                stack(b, 0, 1, 1)
                stack(b, 0, 2, 1)
                spill(b, 1, 1)
                stack(b, 0, 3, 1)
                for g in range(NKV):
                    stack(b, 1, g, 1)

            sp.dma_start(first[:], first_in).then_inc(first_loaded, 16)
            for c in range(NC):
                load_u(0, c)
            for dst, src in ((late, late_in), (bias_in[:, 0:2 * HID], b1), (bias_in[:, 2 * HID:], b2),
                             (w_1, W1.rearrange("e p f -> p e f")), (w_2, W2.rearrange("e (k p) d -> p e k d", p=P))):
                sp.dma_start(dst[:], src).then_inc(late_loaded, 16)
            sp.wait_ge(x1_kept, 1)
            load_u(1, 0)
            sp.wait_ge(zeroed, 1)
            spill(0, 0)
            stack(0, 0, 0)
            sp.wait_ge(x1_kept, 2)
            load_u(1, 1)
            for g in range(1, NKV):
                stack(0, 0, g)
            spill(0, 1)
            for g in range(NKV):
                stack(0, 1, g)
            spare = xs_rows[SPARE:ROWS, :].rearrange("(n p) d -> p n d", p=P)
            sp.dma_start(spare, zero_rows[:].unsqueeze(1).to_broadcast([P, ENTRIES - FULL, ROW])).then_inc(filled, 16)
            with sp.Fori(0, B - 2) as b:
                body(b, True)
            body(B - 2, False)
            fill(sp, range(0, E, 2))
            sp.wait_ge(rows_ready, 1)
            sp.wait_ge(scattered, 16 * B * NT)
            sp.wait_ge(filled, 16 * (E + 1))

            def load(k, j, it):
                need(sp, z_ready, k - RING + 1)
                r = sp.value_load(tile_row[0:1, bass.ds(k, 1)], min_val=0, max_val=ROWS - P)
                sp.dma_start(x_in[:, j, :], xs_rows[bass.ds(r, P), :]).then_inc(x_loaded[j], 16)
            over_tiles(sp, load)
            for j in range(ENTRIES - TILES):
                load(TILES + j, j, TILES // RING)
            for j in range(RING):
                sp.wait_ge(out_stored[j], 16 * (TILES // RING))

        @block.gpsimd
        def _(pool):
            state = dict(n=0, b=None, per=0)

            def link(ins):
                ins.then_inc(pool_step, 1)
                state["n"] += 1
                pool.wait_ge(pool_step, state["n"] if state["b"] is None else state["b"] * state["per"] + state["n"])

            def hold():
                pool.sem_inc(pool_held, 1)

            def piece(kind, at, run, name):
                L = fillings(kind, at, run)
                b, c = at + RUNS[run][0], RUNS[run][1]
                cc = b * NC + c
                span = slice(CH * c, CH * c + CH)
                if name == "qkv23":
                    read_bank(pool, L["qkv01"])
                    read_bank(pool, L["qkv23"])
                    pool.wait_ge(v_copied, b * NKV)
                    hold()
                    nc.gpsimd.tensor_copy(v_next[:, TQ * c:TQ * c + TQ, :], qkv[:, :, QW + KW:]).then_inc(v_kept, 1)
                elif name == "h2T":
                    pool.wait_ge(h2_ready, cc + 1)
                    hold()
                    tiles = resid[:, bass.ds(b * NT + TQ * c, TQ), :]
                    nc.gpsimd.tensor_tensor(last_resid, tiles, x2[:], ALU.add).then_inc(x2_kept, 1)
                elif name.startswith("scatter"):
                    q = int(name[-1])
                    if q == 0:
                        pool.wait_ge(slot_ready, cc + 1)
                        pool.wait_ge(x2_kept, cc + 1)
                        hold()
                    nc.gpsimd.indirect_dma_start(
                        xs_rows, bass.IndirectOffsetOnAxis(ap=slot[:, q:q + 1], axis=0),
                        routed[:, q, :], None).then_inc(scattered, 16)

            def copy_v(b, g):
                pool.wait_ge(v_kept, b * NC + NC)
                if not (isinstance(b, int) and b == 0):
                    pool.wait_ge(probs_used, (b - 1) * NU + LAST[NC - 1, g] + 1 + PROBS)
                hold()
                nc.gpsimd.tensor_copy(v_pad[:, :, g, 0:HD], v_next[:, :, HD * g:HD * g + HD]).then_inc(v_copied, 1)

            def copy_first_v(c):
                pool.wait_ge(v_kept, c + 1)
                tiles = slice(TQ * c, TQ * c + TQ)
                nc.gpsimd.tensor_copy(v_pad[:, tiles, :, 0:HD], v_next[:, tiles, :].rearrange("p t (g d) -> p t g d", d=HD)) \
                    .then_inc(*((first_v1_copied, 1) if c else (v_copied, NKV)))

            def mask(b, u):
                if not UNITS[u]["diag"]:
                    return
                pool.wait_ge(scores_read, b * NS + UNITS[u]["subs"][-1] + 1 + 2)
                pr = probs[:, u % PROBS, :, 0:P]
                hold()
                nc.gpsimd.affine_select(out=pr, in_=pr, pattern=[[0, GH], [1, P]], compare_op=ALU.is_ge,
                                        fill=0.0, base=0, channel_multiplier=-1).then_inc(probs_masked, 1)

            def body(kind, b):
                for u in range(NU):
                    if u + 1 < NU:
                        mask(b, u + 1)
                    elif kind != "last":
                        mask(b + 1, 0)
                    if u == 2 and kind != "first":
                        copy_v(b, NKV - 1)
                    if u == LAST[NC - 1, NKV - 2] + 2 and kind != "last":
                        for g in range(NKV - 1):
                            copy_v(b + 1, g)
                    for run, name in PLANS[kind][u]:
                        piece(kind, b, run, name)
                        if (run, name) == ("P1", "qkv23"):
                            copy_first_v(1)

            link(nc.gpsimd.memset(qT[:], 0.0))
            link(nc.gpsimd.memset(kT[:], 0.0))
            link(nc.gpsimd.memset(zero_rows[:], 0.0))
            link(nc.gpsimd.memset(routed[:, :, 2 * D + 1:], 0.0))
            link(nc.gpsimd.memset(v_pad[:], 0.0))
            nc.gpsimd.memset(v_pad[:, :, :, HD:HD + 1], 1.0).then_inc(zeroed, 1)
            for run, name in PRO:
                piece("before", -1, run, name)
            copy_first_v(0)
            mask(0, 0)
            body("first", 0)
            with pool.Fori(1, B - 1) as b:
                body("steady", b)
            body("last", B - 1)
            for run, name in EPI:
                piece("after", B, run, name)

            def store(k, j, it):
                pool.wait_ge(out_ready, (it + 1) * (RING // PAIR) + j // PAIR + 1)
                hold()
                nc.gpsimd.indirect_dma_start(
                    out, bass.IndirectOffsetOnAxis(ap=number_out[:, j:j + 1], axis=0), z_out[:, j, :], None).then_inc(out_stored[j], 16)
            over_tiles(pool, store)

        @block.scalar
        def _(act):
            act.dma_start(second[:], second_in).then_inc(second_loaded, 16)
            act.wait_ge(first_loaded, 16)
            act.sem_inc(scores_read, 2)
            nc.scalar.activation(lam[:], log_lam[:], ACT.Exp, scale=-1.0).then_inc(exp_neg, 1)
            act.wait_ge(lam_ready, 1)

            def piece(kind, at, run, name):
                L = fillings(kind, at, run)
                b, c = at + RUNS[run][0], RUNS[run][1]
                cc = b * NC + c
                if name in ("up0", "up1"):
                    k = int(name[-1])
                    filled_bank(act, L[name])
                    nc.scalar.activation(xs[:, c, k, :], M[L[name][0]][:], ACT.Copy,
                                         scale=one_minus_lam[:, k:k + 1]).then_inc(misc_read[L[name][0]], 1)
                elif name == "x1T":
                    filled_bank(act, L[name])
                    nc.scalar.activation(x1T[:], M[L[name][0]][:], ACT.Copy).then_inc(misc_read[L[name][0]], 1)
                elif name == "qT":
                    act.wait_ge(parts_ready, cc)
                    filled_bank(act, L[name])
                    nc.scalar.activation(q_scaled[:], M[L[name][0]][:], ACT.Copy, scale=qn_col[:]).then_inc(misc_read[L[name][0]], 1)
                elif name == "kT":
                    filled_bank(act, L[name])
                    nc.scalar.activation(k_scaled[:], M[L[name][0]][0:KW, :], ACT.Copy,
                                         scale=kn_col[:]).then_inc(misc_read[L[name][0]], 1)
                elif name == "gate":
                    act.wait_ge(gate_ready, cc + 1)
                    g = gate[:].rearrange("p q h d -> p (q h d)")
                    nc.scalar.activation(g, g, ACT.Tanh, scale=0.5).then_inc(gate_tanh, 1)
                elif name == "ogT":
                    filled_bank(act, L[name])
                    nc.scalar.activation(ogT[:], M[L[name][0]][:], ACT.Copy).then_inc(misc_read[L[name][0]], 1)
                elif name == "h2T":
                    filled_bank(act, L[name])
                    nc.scalar.activation(h2T[:], M[L[name][0]][:], ACT.Copy).then_inc(misc_read[L[name][0]], 1)

            def exps(b, u):
                w = UNITS[u]["w"]
                act.wait_ge(probs_used, b * NU + u + 1)
                for n in UNITS[u]["subs"]:
                    hs = SUBS[n][1]
                    act.wait_ge(scores_ready, b * NS + n + 1)
                    dst = probs[:, u % PROBS, hs[0]:hs[-1] + 1, 0:w]
                    two = S2[n % 2]
                    if w > CH // 2:
                        src = two[:, :, 0:w]
                    elif w == CH // 2:
                        src = two[:, :, :].rearrange("p a (h w) -> p (a h) w", w=w)
                    else:
                        src = two[:, 0, :].rearrange("p (h w) -> p h w", w=w)
                    nc.scalar.activation(dst, src, ACT.Exp, bias=shift[:], scale=float(HD) ** -0.5).then_inc(scores_read, 1)

            def body(kind, b):
                for u in range(NU):
                    if u + 1 < NU:
                        exps(b, u + 1)
                    elif kind != "last":
                        exps(b + 1, 0)
                    if u:
                        keep_outputs(b, u - 1)
                    elif kind != "first":
                        keep_outputs(b - 1, NU - 1)
                    for run, name in PLANS[kind][u]:
                        piece(kind, b, run, name)

            def keep_outputs(b, u):
                unit = UNITS[u]
                if unit["last"]:
                    act.wait_ge(probs_used, b * NU + u + 1 + PROBS)
                    nc.scalar.activation(oT[:, unit["g"], CH * unit["c"]:CH * unit["c"] + CH], O[unit["out"] % 2][:],
                                         ACT.Copy).then_inc(o_read, 1)

            for run, name in PRO:
                if (run, name) == ("A1", "x1T"):
                    act.wait_ge(bias_split_ready, 1)
                    for p in range(PARTS):
                        act.dma_start(bias[p:p + 1, :, :], bias_split[:, p, :]).then_inc(bias_ready, 16)
                piece("before", -1, run, name)
            act.wait_ge(late_ready, 1)
            act.wait_ge(bias_ready, 16 * PARTS)
            exps(0, 0)
            body("first", 0)
            with act.Fori(1, B - 1) as b:
                body("steady", b)
            body("last", B - 1)
            keep_outputs(B - 1, NU - 1)
            for run, name in EPI:
                piece("after", B, run, name)

            def tile_step(k, j, it):
                i = j % 2
                act.wait_ge(up_ready, k + 1)
                need(act, hid_ready, k - 1)
                nc.scalar.activation(sig[:, i, :], PU[i][:, HID:], ACT.Sigmoid).then_inc(sig_ready, 1)
                if not isinstance(k, int) or k >= 1:
                    turned(k - 1, (j - 1) % 2)
                turn_at(k + 2, j % 2)

            def turned(k, i):
                act.wait_ge(hid_turned, k + 1)
                need(act, y_ready, k - 1)
                nc.scalar.activation(hidT[:, i, :], PH[i][:, 0:HID], ACT.Copy).then_inc(hidT_ready, 1)

            def turn_at(k, i):
                need(act, up_ready, k - 1)
                act.wait_ge(x_turned, k + 1)
                nc.scalar.activation(xT[:, i, :], PX[i][:, 0:P], ACT.Copy).then_inc(xT_ready, 1)

            fill(act, range(1, E, 2))
            act.wait_ge(table_ready, 1)
            turn_at(0, 0)
            turn_at(1, 1)
            over_tiles(act, tile_step)
            turned(TILES - 1, (TILES - 1) % 2)

        @block.vector
        def _(dve):
            v = nc.vector
            state = dict(n=0, b=None, per=0)

            def link(ins):
                ins.then_inc(dve_step, 1)
                state["n"] += 1
                dve.wait_ge(dve_step, state["n"] if state["b"] is None else state["b"] * state["per"] + state["n"])

            def rsqrt(y, x, tmp):
                first_guess(y, x)
                for _ in range(3):
                    newton(y, x, tmp)

            def first_guess(y, x):
                link(v.tensor_scalar(y.bitcast(I32), x.bitcast(I32), -0.5, RSQRT_MAGIC, ALU.mult, ALU.add))

            def newton(y, x, tmp):
                link(v.scalar_tensor_tensor(tmp, y, -0.5, y, ALU.mult, ALU.mult))
                link(v.tensor_tensor(tmp, tmp, x, ALU.mult))
                link(v.scalar_tensor_tensor(y, tmp, 1.5, y, ALU.add, ALU.mult))

            dve.sem_inc(o_read, 2)
            dve.sem_inc(out_ready, RING // PAIR)
            v.memset(ones_bf[:], 1.0)
            v.memset(seen[:], 0.0)
            v.memset(no_tokens[:], 0.0)
            dve.wait_ge(first_loaded, 16)
            dve.wait_ge(exp_neg, 1)
            link(v.tensor_scalar(lam[:], lam[:], 1.0, None, ALU.add))
            link(v.reciprocal(lam[:], lam[:]))
            v.tensor_scalar(one_minus_lam[:], lam[:], -1.0, 1.0, ALU.mult, ALU.add).then_inc(lam_ready, 1)
            link(v.tensor_scalar(d_col[:], d_col[:], 1.0, None, ALU.add))
            v.tensor_scalar(skip_diag[:], idm[:], d_col[:], None, ALU.mult)
            dve.wait_ge(second_loaded, 16)
            v.tensor_scalar(w_qkv[:], w_qkv[:], ln1_col[:], None, ALU.mult).then_inc(w_scaled, 1)

            def late_constants():
                dve.wait_ge(late_loaded, 16 * LATE_DMAS)
                link(v.tensor_copy(bias_split[:, 0, :], bias_in[:]))
                link(v.tensor_tensor(bias_rest[:], bias_in[:], bias_split[:, 0, :], ALU.subtract))
                link(v.tensor_copy(bias_split[:, 1, :], bias_rest[:]))
                v.tensor_tensor(bias_split[:, 2, :], bias_rest[:], bias_split[:, 1, :], ALU.subtract).then_inc(bias_split_ready, 1)
                v.tensor_scalar(w_r[:], w_r[:], ln2_col[:], None, ALU.mult)
                link(v.tensor_tensor(bound[:], norm_rows[:, 0, :], norm_rows[:, 1, :], ALU.mult))
                link(v.scalar_tensor_tensor(bound[:], bound[:], -1.0, bound[:], ALU.mult, ALU.max))
                link(v.tensor_reduce(shift[:], bound[:], AX_X, ALU.max))
                link(v.tensor_scalar(shift[:], shift[:], -float(HD) ** 0.5, SHIFT_FROM, ALU.mult, ALU.add))
                v.tensor_scalar(shift[:], shift[:], 0.0, None, ALU.min).then_inc(late_ready, 1)

            def stage_a(L, b, c, name):
                cc = b * NC + c
                if name in ("up0", "up1"):
                    k = int(name[-1])
                    if c:
                        dve.wait_ge(scan_done, cc * SH + (k + 1 - SH))
                    read_bank(dve, L[name])
                    v.tensor_tensor_scan(xs[:, c, k, :], lam[:, k:k + 1].to_broadcast([P, CH]), xs[:, c, k, :],
                                         0.0 if c == 0 else xs[:, c - 1, k, CH - 1:CH],
                                         ALU.mult, ALU.add).then_inc(scan_done, 1)
                elif name == "z":
                    z = M[L[name][0]]
                    filled_bank(dve, L[name])
                    for q in range(TQ):
                        ins = v.bn_stats(stats[:, q, :], z[:, P * q:P * q + P])
                    link(ins)
                    dve.sem_inc(dve_held, 1)
                    for q in range(TQ):
                        ins = v.bn_aggr(mv[:, q, :], stats[:, q, :])
                    link(ins)
                    v.tensor_scalar(ln_arg[:, 0:TQ], mv[:, :, 1], LN_EPS, None, ALU.add)
                    link(v.tensor_scalar(ln_arg[:, TQ:], mv[:, :, 1], 1.0 + RMS_EPS, LN_EPS * RMS_EPS, ALU.mult, ALU.add))
                    rsqrt(ln_rs[:], ln_arg[:], ln_tmp[:])
                    dve.wait_ge(x1_kept, cc)
                    for q in range(TQ):
                        ins = v.tensor_scalar(x1[:, q, :], z[:, P * q:P * q + P], mv[:, q, 0:1], ln_rs[:, q:q + 1],
                                              ALU.subtract, ALU.mult)
                    ins.then_inc(misc_read[L[name][0]], 1)
                    link(v.tensor_tensor(r1[:], ln_arg[:, 0:TQ], ln_rs[:, 0:TQ], ALU.mult))
                    link(v.tensor_tensor(r1[:], r1[:], ln_rs[:, TQ:], ALU.mult))
                    v.tensor_copy(resid[:, bass.ds(b * NT + TQ * c, TQ), :], x1[:]).then_inc(x1_kept, 1)
                elif name in ("qkv01", "qkv23"):
                    q0, w3, m = int(name[3]), QW + 2 * KW, M[L[name][0]]
                    dve.wait_ge(v_kept, cc)
                    filled_bank(dve, L[name])
                    for q in (q0, q0 + 1):
                        ins = v.scalar_tensor_tensor(qkv[:, q, :], m[:, w3 * (q - q0):w3 * (q - q0) + w3],
                                                     r1[:, q:q + 1], b_qkv[:], ALU.mult, ALU.add)
                    ins.then_inc(misc_read[L[name][0]], 1)
                    if name == "qkv23":
                        rope_and_norm(L, b, c)
                elif name == "kT":
                    span = slice(CH * c, CH * c + CH)
                    read_bank(dve, L["qT"])
                    read_bank(dve, L["kT"])
                    dve.wait_ge(spilled[c], b * SPILL)
                    both = ((q_scaled, q_parts), (k_scaled, k_parts))
                    for p in range(PARTS - 1):
                        for x, parts in both:
                            ins = v.tensor_copy(parts[:, p, span], x[:])
                        link(ins)
                        for x, parts in both:
                            dst = x[:] if p < PARTS - 2 else parts[:, PARTS - 1, span]
                            ins = v.tensor_tensor(dst, x[:], parts[:, p, span], ALU.subtract)
                        if p < PARTS - 2:
                            link(ins)
                    ins.then_inc(parts_ready, 1)

            def rope_and_norm(L, b, c):
                read_bank(dve, L["qkv01"])
                read_bank(dve, L["qkv23"])
                head = [P, TQ, NQ + NKV, HD]
                by_head = lambda ap: ap.rearrange("p q (h d) -> p q h d", d=HD)
                qk, ra, rb = by_head(qkv[:, :, 0:QW + KW]), by_head(rot_a[:]), by_head(rot_b[:])
                cos = cos_t[:, TQ * c:TQ * c + TQ, :].unsqueeze(2).to_broadcast(head)
                sin = sin_t[:, TQ * c:TQ * c + TQ, :].unsqueeze(2).to_broadcast(head)
                v.tensor_tensor(ra, qk, cos, ALU.mult)
                v.tensor_tensor(rb[:, :, :, 0:4], qk[:, :, :, 4:8], sin[:, :, :, 0:4], ALU.mult)
                link(v.tensor_tensor(rb[:, :, :, 4:8], qk[:, :, :, 0:4], sin[:, :, :, 4:8], ALU.mult))
                link(v.tensor_tensor(rot_a[:], rot_a[:], rot_b[:], ALU.add))
                link(v.tensor_tensor(rot_b[:], rot_a[:], rot_a[:], ALU.mult))
                link(v.tensor_reduce(hs_arg[:], rot_b[:].rearrange("p q (h d) -> p (q h) d", d=HD), AX_X, ALU.add))
                link(v.tensor_scalar(hs_arg[:], hs_arg[:], 1.0 / HD, RMS_EPS, ALU.mult, ALU.add))
                rsqrt(hs_rs[:], hs_arg[:], hs_tmp[:])
                rs = hs_rs[:].rearrange("p (q h) -> p q h", q=TQ).unsqueeze(3)
                v.tensor_tensor(by_head(qn[:]), ra[:, :, 0:NQ, :], rs[:, :, 0:NQ, :].to_broadcast([P, TQ, NQ, HD]), ALU.mult)
                v.tensor_tensor(by_head(kn[:]), ra[:, :, NQ:, :],
                                rs[:, :, NQ:, :].to_broadcast([P, TQ, NKV, HD]), ALU.mult).then_inc(qkn_ready, 1)

            def stage_c(L, b, c, name):
                cc = b * NC + c
                g = gate[:].rearrange("p q h d -> p q (h d)")
                if name in ("row0", "row1", "row2", "row3"):
                    q, bank = int(name[-1]), L[name][0]
                    m = M[bank][:, 0:NKV * RCOLS].rearrange("p (g x) -> p g x", x=RCOLS)
                    heads = m[:, :, 0:GH * RH].rearrange("p g (j y) -> p g j y", y=RH)
                    filled_bank(dve, L[name])
                    rd = r_den[:, q].rearrange("p (g j) -> p g j", j=GH)
                    link(v.reciprocal(rd, m[:, :, GH * RH:]))
                    rd = rd.unsqueeze(3).to_broadcast([P, NKV, GH, HD])
                    v.tensor_tensor(o_n[:, q].rearrange("p (g j) d -> p g j d", j=GH), heads[:, :, :, 0:HD], rd, ALU.mult)
                    v.tensor_tensor(gate[:, q].rearrange("p (g j) d -> p g j d", j=GH), heads[:, :, :, HD:], rd,
                                    ALU.mult).then_inc(misc_read[bank], 1)
                    if q == TQ - 1:
                        for name in ("row2", "row3"):
                            read_bank(dve, L[name])
                        v.tensor_tensor(g, g, bg_b[:].unsqueeze(1).to_broadcast([P, TQ, QW]),
                                        ALU.add).then_inc(gate_ready, 1)
                elif name == "gate":
                    dve.wait_ge(gate_tanh, cc + 1)
                    v.scalar_tensor_tensor(og[:], g, 1.0, o_n[:].rearrange("p q h d -> p q (h d)"),
                                           ALU.add, ALU.mult).then_inc(og_ready, 1)
                elif name == "proj":
                    tiles = bass.ds(b * NT + TQ * c, TQ)
                    dve.wait_ge(x1_kept, cc + 1)
                    dve.wait_ge(x2_kept, cc)
                    filled_bank(dve, L[name])
                    v.tensor_tensor(x2[:], M[L[name][0]][:].rearrange("p (q d) -> p q d", d=D), resid[:, tiles, :],
                                    ALU.add).then_inc(misc_read[L[name][0]], 1)
                    read_bank(dve, L[name])
                    link(v.tensor_tensor(x2[:], x2[:], bo_b[:].unsqueeze(1).to_broadcast([P, TQ, D]), ALU.add))
                    link(v.tensor_tensor(sq[:], x2[:], x2[:], ALU.mult))
                    link(v.tensor_reduce(r2_arg[:], sq[:], AX_X, ALU.add))
                    link(v.tensor_scalar(r2_arg[:], r2_arg[:], 1.0 / D, RMS_EPS, ALU.mult, ALU.add))
                    rsqrt(r2[:], r2_arg[:], r2_tmp[:])
                    dve.wait_ge(scattered, cc * (16 * TQ))
                    v.tensor_tensor(h2, x2[:], r2[:].unsqueeze(2).to_broadcast([P, TQ, D]),
                                    ALU.mult).then_inc(h2_ready, 1)
                    v.tensor_copy(number, token_no[:, tiles].unsqueeze(2))
                elif name == "logits":
                    filled_bank(dve, L[name])
                    v.tensor_tensor(lg[:], M[L[name][0]][:, 0:TQ * E].rearrange("p (q e) -> p q e", e=E),
                                    br_b[:].unsqueeze(1).to_broadcast([P, TQ, E]), ALU.add).then_inc(misc_read[L[name][0]], 1)
                    read_bank(dve, L[name])
                    top = lg_max[:].unsqueeze(2).to_broadcast([P, TQ, E])
                    link(v.tensor_reduce(lg_max[:], lg[:], AX_X, ALU.max))
                    link(v.tensor_tensor(lg[:], lg[:], top, ALU.is_ge))
                    link(v.tensor_tensor(lg[:], lg[:], rank8[:].unsqueeze(1).to_broadcast([P, TQ, E]), ALU.mult))
                    link(v.tensor_reduce(lg_max[:], lg[:], AX_X, ALU.max))
                    link(v.tensor_tensor(onehot[:], lg[:], top, ALU.is_equal))
                    for q in range(TQ + 1):
                        ins = v.tensor_tensor(seen[:, q, :], seen[:, (q - 1) % (TQ + 1), :],
                                              onehot[:, q - 1, :] if q else no_tokens[:], ALU.add)
                        if q < TQ:
                            link(ins)
                    ins.then_inc(route_ready, 1)
                elif name == "rank":
                    filled_bank(dve, L[name])
                    v.tensor_tensor(slot_f[:], M[L[name][0]][:, 0:TQ * E].rearrange("p (q e) -> p q e", e=E),
                                    region_of[:].unsqueeze(1).to_broadcast([P, TQ, E]), ALU.add).then_inc(misc_read[L[name][0]], 1)
                    read_bank(dve, L[name])
                    link(v.tensor_tensor(slot_f[:], slot_f[:], onehot[:], ALU.mult))
                    link(v.tensor_reduce(slot_s[:], slot_f[:], AX_X, ALU.add))
                    dve.wait_ge(scattered, cc * (16 * TQ))
                    dve.sem_inc(dve_held, 1)
                    v.tensor_copy(slot[:], slot_s[:]).then_inc(slot_ready, 1)

            def piece(kind, at, run, name):
                L = fillings(kind, at, run)
                b, c = at + RUNS[run][0], RUNS[run][1]
                if run[0] in "AP":
                    stage_a(L, b, c, name)
                else:
                    stage_c(L, b, c, name)

            def body(kind, b):
                for u in range(NU):
                    for run, name in PLANS[kind][u]:
                        piece(kind, b, run, name)

            for run, name in PRO:
                if (run, name) == ("A1", "z"):
                    late_constants()
                piece("before", -1, run, name)
            body("first", 0)
            base = state["n"]
            with dve.Fori(1, B - 1) as b:
                state.update(n=base - DVE_STEPS, b=b, per=DVE_STEPS)
                body("steady", b)
                assert state["n"] == base, state["n"] - base
            state.update(n=base + (B - 2) * DVE_STEPS, b=None)
            w1f = w_1[:].rearrange("p e f -> p (e f)")
            v.tensor_scalar(w1f, w1f, ln2_col[:], None, ALU.mult)
            body("last", B - 1)
            for run, name in EPI:
                piece("after", B, run, name)
            dve.wait_ge(count_ready, 1)
            link(v.tensor_copy(count[:], PY[1][:, 0:E]))
            v.tensor_tensor(fill_row[:], count[0:1, :], region_of[0:1, :], ALU.add).then_inc(fill_ready, 1)
            dve.wait_ge(fill_ready, 1)
            over3 = [P, E, FULL]
            link(v.tensor_scalar(count[:], count[:], 1.0 / P, None, ALU.mult))
            link(v.tensor_tensor(over[:], count[:].unsqueeze(2).to_broadcast(over3),
                                 tile_steps[:].unsqueeze(1).to_broadcast(over3), ALU.is_gt))
            link(v.tensor_reduce(n_tiles[:], over[:], AX_X, ALU.add))
            link(v.tensor_tensor_scan(end_tile[:], ones_sq[:, 0:E], n_tiles[:], 0.0, ALU.mult, ALU.add))
            link(v.tensor_tensor(start_tile[:], end_tile[:], n_tiles[:], ALU.subtract))
            link(v.scalar_tensor_tensor(region_a[:], start_tile[0:1, :], -float(P), region_of[0:1, :], ALU.mult, ALU.add))
            link(v.tensor_scalar(region_a[:], region_a[:], -float(SPARE_BASE), None, ALU.add))
            each = [1, ENTRIES, E]
            k3 = tile_no[:].unsqueeze(2).to_broadcast(each)
            link(v.tensor_tensor(mine[:], k3, start_tile[0:1, :].unsqueeze(1).to_broadcast(each), ALU.is_ge))
            link(v.tensor_tensor(mine_x[:], k3, end_tile[0:1, :].unsqueeze(1).to_broadcast(each), ALU.is_ge))
            link(v.tensor_tensor(mine[:], mine[:], mine_x[:], ALU.subtract))
            link(v.tensor_tensor(mine_x[:], mine[:], region_a[0:1, :].unsqueeze(1).to_broadcast(each), ALU.mult))
            link(v.tensor_reduce(row_f[:], mine_x[:], AX_X, ALU.add))
            link(v.scalar_tensor_tensor(row_f[:], tile_no[:], float(P), row_f[:], ALU.mult, ALU.add))
            link(v.tensor_scalar(row_f[:], row_f[:], float(SPARE_BASE), None, ALU.add))
            v.tensor_copy(tile_row[:], row_f[:]).then_inc(rows_ready, 1)
            link(v.tensor_tensor(mine_x[:], mine[:], expert_no[:].unsqueeze(1).to_broadcast(each), ALU.mult))
            link(v.tensor_reduce(exp_f[:], mine_x[:], AX_X, ALU.add))
            v.tensor_copy(tile_expert[:], exp_f[:]).then_inc(table_ready, 1)
            def gated(k, i):
                dve.wait_ge(sig_ready, k + 1)
                need(dve, hid_turned, k - 1)
                v.tensor_tensor(hid[:, i, :], PU[i][:, 0:HID], sig[:, i, :], ALU.mult).then_inc(hid_ready, 1)

            def result(k, j, it):
                dve.wait_ge(y_ready, k + 1)
                dve.wait_ge(out_ready, it * (RING // PAIR) + j // PAIR + 1)
                dve.sem_inc(dve_held, 1)
                v.tensor_copy(number_kept[:, j:j + 1], x_number[:, j, :])
                v.tensor_tensor(z[:, j, :], PY[j % 2][:, 0:D], x_in[:, j, D:2 * D], ALU.add).then_inc(z_ready, 1)

            def norm(n, g, it, tile0):
                tiles = range(g * GROUP, g * GROUP + GROUP)
                span = slice(g * GROUP, g * GROUP + GROUP)
                arg, y, tmp = z_arg[:, span], z_rs[:, span], z_tmp[:, span]
                if n:
                    after_step()
                if n == 0:
                    dve.wait_ge(z_counted, tile0 + GROUP)
                    dve.sem_inc(dve_held, 1)
                    for j in tiles:
                        ins = v.bn_aggr(z_mv[:, j, :], z_stats[:, j, :])
                elif n == 1:
                    ins = v.tensor_scalar(arg, z_mv[:, span, 1], LN_EPS, None, ALU.add)
                elif n == 2:
                    ins = v.tensor_scalar(y.bitcast(I32), arg.bitcast(I32), -0.5, RSQRT_MAGIC, ALU.mult, ALU.add)
                elif n < 12 and n % 3 == 0:
                    ins = v.scalar_tensor_tensor(tmp, y, -0.5, y, ALU.mult, ALU.mult)
                elif n < 12 and n % 3 == 1:
                    ins = v.tensor_tensor(tmp, tmp, arg, ALU.mult)
                elif n < 12:
                    ins = v.scalar_tensor_tensor(y, tmp, 1.5, y, ALU.add, ALU.mult)
                elif n == 12:
                    ins = v.scalar_tensor_tensor(number_spare[:, span], number_kept[:, span], 0.0,
                                                 token_no[:, bass.ds(tile0 + B * NT, GROUP)], ALU.is_equal, ALU.mult)
                elif n == 13:
                    for j in tiles:
                        need(dve, out_stored[j], it * 16 - 16)
                    dve.sem_inc(dve_held, 1)
                    ins = v.tensor_tensor(number_out[:, span], number_spare[:, span], number_kept[:, span], ALU.add)
                else:
                    for j in tiles[(n - 14) * PAIR:(n - 14) * PAIR + PAIR]:
                        ins = v.tensor_scalar(z_out[:, j, :], z[:, j, :], z_mv[:, j, 0:1], z_rs[:, j:j + 1],
                                              ALU.subtract, ALU.mult)
                    ins.then_inc(out_ready, 1)
                    return
                ins.then_inc(dve_step, 1)
                state["n"] += 1

            def after_step():
                dve.wait_ge(dve_step, state["n"] if state["b"] is None else state["b"] * state["per"] + state["n"])

            def measure(k, j):
                dve.wait_ge(z_ready, k + 1)
                v.bn_stats(z_stats[:, j, :], z[:, j, :]).then_inc(z_counted, 1)

            def tile_step(k, j, it):
                first = isinstance(k, int)
                part = (j - GROUP + 1) % GROUP
                tile0 = k - part - GROUP - (GROUP - 1)

                def some(i):
                    if not first or 0 <= tile0 < TILES:
                        norm(part * (NORM_OPS // GROUP) + i, (j - GROUP - part) % RING // GROUP, it, tile0)

                some(0)
                if not first or 3 <= k <= TILES + 2:
                    measure(k - 3, (j - 3) % RING)
                some(1)
                if not first or k < TILES:
                    gated(k, j % 2)
                some(2)
                some(3)
                if not first or 2 <= k <= TILES + 1:
                    result(k - 2, (j - 2) % RING, it + (j - 2) // RING)

            base = state["n"]
            for k in range(2 * RING):
                tile_step(k, k % RING, k // RING)
            base = state["n"]
            with dve.Fori(2, TILES // RING) as it:
                state.update(n=base - 2 * TILE_STEPS, b=it, per=TILE_STEPS)
                for j in range(RING):
                    tile_step(it * RING + j, j, it)
                assert state["n"] == base - TILE_STEPS, state["n"] - base
            state.update(n=base + (TILES // RING - 2) * TILE_STEPS, b=None)
            for k in range(TILES, TILES + 2 * GROUP - 1):
                tile_step(k, k % RING, TILES // RING)

        @block.tensor
        def _(pe):
            mm = nc.tensor.matmul
            pe.wait_ge(first_loaded, 16)
            pe.sem_inc(probs_used, PROBS)
            turn_tiles = lambda dst, src: [nc.tensor.transpose(dst[:, P * q:P * q + P], src[:, q, :], idm[:]) for q in range(TQ)][-1]

            def stage_a(L, b, c, name):
                cc = b * NC + c
                m, full = M[L[name][0]], misc_full[L[name][0]]
                if name in ("up0", "up1"):
                    k = int(name[-1])
                    pe.wait_ge(u_loaded[c], b * 16 + 16)
                    free_bank(pe, L[name])
                    mm(m[:], w_in[:, P * k:P * k + P], u_sb[:, c, :], start=True, stop=True).then_inc(full, 1)
                elif name == "z":
                    pe.wait_ge(scan_done, cc * SH + SH)
                    free_bank(pe, L[name])
                    for q in range(TQ):
                        tok = slice(P * q, P * q + P)
                        for k in range(SH):
                            mm(m[:, tok], xs[:, c, k, tok], w_out[:, k, :], start=k == 0, stop=False)
                        ins = mm(m[:, tok], u_sb[:, c, tok], skip_diag[:], start=False, stop=True)
                    ins.then_inc(full, 1)
                elif name == "x1T":
                    read_bank(pe, L["z"])
                    free_bank(pe, L[name])
                    turn_tiles(m, x1).then_inc(full, 1)
                elif name in ("qkv01", "qkv23"):
                    q0, w3 = int(name[3]), QW + 2 * KW
                    read_bank(pe, L["x1T"])
                    free_bank(pe, L[name])
                    for q in (q0, q0 + 1):
                        ins = mm(m[:, w3 * (q - q0):w3 * (q - q0) + w3], x1T[:, P * q:P * q + P], w_qkv[:], start=True, stop=True)
                    ins.then_inc(full, 1)
                elif name == "qT":
                    pe.wait_ge(qkn_ready, cc + 1)
                    free_bank(pe, L[name])
                    turn_tiles(m, qn).then_inc(full, 1)
                elif name == "kT":
                    free_bank(pe, L[name])
                    turn_tiles(m[0:KW, :], kn).then_inc(full, 1)

            def stage_c(L, b, c, name):
                cc = b * NC + c
                m, full = M[L[name][0]], misc_full[L[name][0]]
                if name in ("row0", "row1", "row2", "row3"):
                    q = int(name[-1])
                    pe.wait_ge(o_read, b * NO + NKV * (c + 1) + 2)
                    free_bank(pe, L[name])
                    for g in range(NKV):
                        t = CH * c + P * q
                        ins = mm(m[:, RCOLS * g:RCOLS * g + RCOLS], oT[:, g, t:t + P], mix[:], start=True, stop=True)
                    ins.then_inc(full, 1)
                elif name == "ogT":
                    pe.wait_ge(og_ready, cc + 1)
                    free_bank(pe, L[name])
                    turn_tiles(m, og).then_inc(full, 1)
                elif name == "proj":
                    read_bank(pe, L["ogT"])
                    free_bank(pe, L[name])
                    for q in range(TQ):
                        ins = mm(m[:, P * q:P * q + P], ogT[:, P * q:P * q + P], w_o[:], start=True, stop=True)
                    ins.then_inc(full, 1)
                elif name == "h2T":
                    pe.wait_ge(h2_ready, cc + 1)
                    free_bank(pe, L[name])
                    turn_tiles(m, h2).then_inc(full, 1)
                elif name == "logits":
                    read_bank(pe, L["h2T"])
                    free_bank(pe, L[name])
                    for q in range(TQ):
                        ins = mm(m[:, E * q:E * q + E], h2T[:, P * q:P * q + P], w_r[:], start=True, stop=True)
                    ins.then_inc(full, 1)
                elif name == "rank":
                    pe.wait_ge(route_ready, cc + 1)
                    free_bank(pe, L[name])
                    rank = m[:, 0:TQ * E]
                    mm(rank, before[:], onehot[:].rearrange("p q e -> p (q e)"), start=True, stop=False)
                    mm(rank, ones_sq[:], seen[:, 0:TQ, :].rearrange("p q e -> p (q e)"), start=False, stop=True).then_inc(full, 1)

            def piece(kind, at, run, name):
                if name in BANKLESS:
                    return
                L = fillings(kind, at, run)
                b, c = at + RUNS[run][0], RUNS[run][1]
                if run[0] in "AP":
                    stage_a(L, b, c, name)
                else:
                    stage_c(L, b, c, name)

            def score(b, n):
                u, hs = SUBS[n]
                unit = UNITS[u]
                w, g, c = unit["w"], unit["g"], unit["c"]
                key = kT[:, g, P * unit["i"]:P * unit["i"] + P]
                if unit["first"]:
                    pe.wait_ge(stacked[c][g], b * STACK + STACK)
                pe.wait_ge(scores_read, b * NS + n + 1)
                per_bank = max(1, CH // w)
                for a in range(0, len(hs), per_bank):
                    k = min(per_bank, len(hs) - a)
                    h0 = GH * g + hs[a]
                    dst = S2[n % 2][:, a // per_bank, 0:k * w]
                    ins = mm(dst, key, qT[:, c, h0:h0 + k, CH - w:], start=True, stop=True)
                ins.then_inc(scores_ready, 1)

            def weigh(b, u):
                unit = UNITS[u]
                w, g, c = unit["w"], unit["g"], unit["c"]
                if unit["first"]:
                    pe.wait_ge(o_read, b * NO + unit["out"] + 1)
                    if c == 0:
                        pe.wait_ge(v_copied, b * NKV + g + 1)
                    elif isinstance(b, int) and b == 0:
                        pe.wait_ge(first_v1_copied, 1)
                if unit["diag"]:
                    pe.wait_ge(probs_masked, b * NM + unit["masks_before"] + 1)
                else:
                    pe.wait_ge(scores_read, b * NS + unit["subs"][-1] + 1 + 2)
                for j in range(GH):
                    ins = mm(O[unit["out"] % 2][32 * j:32 * j + 32, CH - w:CH], v_pad[:, unit["i"], g, :], probs[:, u % PROBS, j, 0:w],
                             start=unit["first"], stop=unit["last"], tile_position=(0, 32 * j))
                ins.then_inc(probs_used, 1)

            def body(kind, b):
                for u in range(NU):
                    nb, nu = (b, u + 1) if u + 1 < NU else (b + 1, 0)
                    ahead = UNITS[nu]["subs"] if u + 1 < NU or kind != "last" else []
                    for n in ahead[:1]:
                        score(nb, n)
                    if u:
                        weigh(b, u - 1)
                    elif kind != "first":
                        weigh(b - 1, NU - 1)
                    for n in ahead[1:]:
                        score(nb, n)
                    for run, name in PLANS[kind][u]:
                        piece(kind, b, run, name)

            for run, name in PRO:
                if (run, name) == ("A0", "z"):
                    pe.wait_ge(w_scaled, 1)
                piece("before", -1, run, name)
            pe.wait_ge(late_ready, 1)
            for n in UNITS[0]["subs"]:
                score(0, n)
            body("first", 0)
            with pe.Fori(1, B - 1) as b:
                body("steady", b)
            body("last", B - 1)
            weigh(B - 1, NU - 1)
            for run, name in EPI:
                piece("after", B, run, name)
            mm(PY[1][:, 0:E], ones_sq[:], seen[:, TQ, :], start=True, stop=True).then_inc(count_ready, 1)

            def turn(k, j, it):
                pe.wait_ge(x_loaded[j], it * 16 + 16)
                need(pe, xT_ready, k - 1)
                nc.tensor.transpose(PX[j % 2][:, 0:P], x_in[:, j, 0:D], idm[:]).then_inc(x_turned, 1)

            def up(k, j, e):
                pe.wait_ge(xT_ready, k + 1)
                need(pe, hid_ready, k - 1)
                mm(PU[j % 2], xT[:, j % 2, :], w_1[:, bass.ds(e, 1), :].squeeze(1), start=True, stop=False)
                mm(PU[j % 2], ones_bf[:], bias[:, bass.ds(e, 1), 0:2 * HID].squeeze(1), start=False, stop=True).then_inc(up_ready, 1)

            def turn_hidden(k, j):
                pe.wait_ge(hid_ready, k + 1)
                need(pe, hidT_ready, k - 1)
                for f in range(2):
                    ins = nc.tensor.transpose(PH[j % 2][:, P * f:P * f + P], hid[:, j % 2, P * f:P * f + P], idm[:])
                ins.then_inc(hid_turned, 1)

            def down(k, j, e):
                pe.wait_ge(hidT_ready, k + 1)
                need(pe, z_ready, k - 1)
                y = PY[j % 2][:, 0:D]
                for f in range(2):
                    mm(y, hidT[:, j % 2, P * f:P * f + P], w_2[:, bass.ds(e, 1), f, :].squeeze(1), start=f == 0, stop=False)
                mm(y, ones_bf[:], bias[:, bass.ds(e, 1), 2 * HID:].squeeze(1), start=False, stop=True).then_inc(y_ready, 1)

            def expert(k):
                return pe.value_load(tile_expert[0:1, bass.ds(k, 1)], min_val=0, max_val=E - 1)

            def round_of_tiles(k0, it):
                peeled = isinstance(k0, int)
                experts = {0: expert(k0)}
                for j in range(RING):
                    k = k0 + j
                    up(k, j, experts[j])
                    if j + 1 < RING:
                        experts[j + 1] = expert(k + 1)
                    if not peeled or k >= 1:
                        turn_hidden(k - 1, (j - 1) % RING)
                    if not peeled and j < 2:
                        experts[j - 2] = expert(k - 2)
                    if not peeled or k >= 2:
                        down(k - 2, (j - 2) % RING, experts[j - 2])
                    turn(k + 2, (j + 2) % RING, it + (j + 2) // RING)

            pe.wait_ge(bias_ready, 16 * PARTS)
            pe.wait_ge(table_ready, 1)
            turn(0, 0, 0)
            turn(1, 1, 0)
            round_of_tiles(0, 0)
            with pe.Fori(1, TILES // RING) as it:
                round_of_tiles(it * RING, it)
            last = [expert(TILES - 2), expert(TILES - 1)]
            turn_hidden(TILES - 1, (TILES - 1) % RING)
            for k in (TILES - 2, TILES - 1):
                down(k, k % RING, last[k - (TILES - 2)])


DVE_STEPS = 124
NORM_OPS = 16
TILE_STEPS = 2 * (NORM_OPS - 2)

_ORDER = ["uT", "first", "second", "late", "W1", "b1", "W2", "b2"]


def shape_constants():
    inv_freq = (np.float32(1.0) / np.float32(10000.0) ** (np.arange(0, HD, 2, dtype=np.float32) / np.float32(HD))).astype(np.float32)
    ang = np.arange(T, dtype=np.float32)[:, None] * inv_freq[None, :]
    c, s = np.cos(ang).astype(np.float32), np.sin(ang).astype(np.float32)
    by_tile = lambda a: a.reshape(NT, P, HD).transpose(1, 0, 2)
    tables = {"idm": np.eye(P), "cos_t": by_tile(np.concatenate([c, c], 1)), "sin_t": by_tile(np.concatenate([-s, s], 1)),
            "rank8": np.arange(E, 0, -1), "ones_sq": np.ones((P, P)), "before": np.triu(np.ones((P, P)), 1),
            "region_of": np.arange(E) * REGION, "tile_steps": np.arange(FULL), "tile_no": np.arange(ENTRIES),
            "expert_no": np.arange(E), "token_no": 1 + np.arange(P)[:, None] + P * np.arange(B * NT + TILES)}
    return {k: x.astype(np.float32) for k, x in tables.items()}


def kernel(**inputs):
    import concourse.bacc as bacc
    from concourse.bass_utils import run_bass_kernel_spmd

    a = {k.replace("L0_attn_", "").replace("L0_ffn_", ""): np.asarray(x) for k, x in inputs.items()}
    gate_mix = np.zeros((P, RCOLS), np.float32)
    for j in range(GH):
        gate_mix[32 * j:32 * j + HD, RH * j:RH * j + HD] = np.diag(np.full(HD, 0.5, np.float32))
        gate_mix[32 * j:32 * j + HD, RH * j + HD:RH * j + RH] = a["Wg"]
        gate_mix[32 * j + HD, GH * RH + j] = 1.0
    by_half = lambda x: x.reshape((SH, P) + x.shape[1:]).swapaxes(0, 1)
    column = lambda x: x[:, None]
    parts = {"w_in": a["W_in"].T, "log_lam": by_half(a["log_lambda"]), "d_col": column(a["D"]), "ln1_col": column(a["ln1_w"]),
             "qn_col": column(np.tile(a["qn_w"], NQ)), "kn_col": column(np.tile(a["kn_w"], NQ)),
             "w_out": by_half(a["W_out"].T), "w_qkv": np.concatenate([a["Wq"], a["Wk"], a["Wv"]], 1),
             "b_qkv": np.concatenate([a["bq"], a["bk"], a["bv"]]), "mix": gate_mix, "w_o": a["Wo"], "bo_b": a["bo"],
             "w_r": a["Wr"], "br_b": a["br"], "bg_b": np.tile(a["bg"], NQ), "norm_rows": np.concatenate([a["qn_w"], a["kn_w"]]),
             "ln2_col": column(a["ln2_w"]), **shape_constants()}

    def together(columns):
        rows = [np.broadcast_to(parts[k], (P, n)) if parts[k].ndim == 1 else parts[k].reshape(P, n) for k, n in columns.items()]
        return np.concatenate(rows, 1)

    arrays = {"uT": a["u"].transpose(0, 2, 1), "first": together(FIRST), "second": together(SECOND), "late": together(LATE)}
    for name in _ORDER:
        if name not in arrays:
            arrays[name] = a[name]
    nc = bacc.Bacc("TRN2", target_bir_lowering=False, num_devices=1)
    feed, args = {}, []
    for name in _ORDER:
        x = np.ascontiguousarray(arrays[name])
        feed[f"in_{name}"] = x
        args.append(nc.dram_tensor(f"in_{name}", x.shape, mybir.dt.from_np(x.dtype), kind="ExternalInput").ap())
    out = nc.dram_tensor("out", (1 + TOKENS + TILES * P, D), F32, kind="ExternalOutput").ap()
    block_kernel(nc, *args, out)
    r = run_bass_kernel_spmd(nc, [feed], core_ids=[0])
    got = np.asarray(r.results[0]["out"])
    return got[1:1 + TOKENS].reshape(B, T, D)
```
